# Optimizing a Trainium2 kernel written in Bass

```python
import numpy as np
import jax
import jax.numpy as jnp

def _softmax(x, axis=-1):
    return jax.nn.softmax(x, axis=axis)

def _gelu(x):
    return jax.nn.gelu(x, approximate=True)

def _silu(x):
    return jax.nn.silu(x)

def _sigmoid(x):
    return jax.nn.sigmoid(x)

def _layernorm(x, axis=-1, eps=1e-05):
    m = jnp.mean(x, axis=axis, keepdims=True)
    v = jnp.var(x, axis=axis, keepdims=True)
    return (x - m) / jnp.sqrt(v + eps)

def _scatter_add(tgt, idx, src, axis=0):
    return tgt.at[idx].add(src)

def _segment_sum(src, seg, n):
    return jax.ops.segment_sum(src, seg, n)
kernel_name = 'mk_adj_preln_d2_adj_r2_e70964'

def setup_inputs(seed: int=0):
    np.random.seed(seed)
    _w = jnp.asarray

    def _rec_inputs():
        import jax
        import jax.numpy as jnp
        _gk = jax.random.key(seed)
        x = -0.0005207 + 1.001 * jax.random.normal(jax.random.fold_in(_gk, 1), (4096, 128), jnp.float32)
        _a = jax.random.bernoulli(jax.random.fold_in(_gk, 2), 0.00195312, (4096, 4096))
        _a = jnp.logical_or(_a, jnp.swapaxes(_a, -1, -2))
        _a = jnp.logical_or(_a, jnp.eye(4096, dtype=bool))
        _af = _a.astype(jnp.float32)
        _af = _af * jax.random.uniform(jax.random.fold_in(_gk, 3), (4096, 4096), jnp.float32, 0.05, 2.05)
        adj = _af
        return (x, adj)
    x, adj = _rec_inputs()

    def _L0_gnn_setup():
        import jax, jax.numpy as jnp
        import numpy as np
        N = 4096
        D = 128
        CUTOFF = 1.0
        MU = 1.0
        SIGMA = 0.5

        def sensitivity(r, mu, sigma):
            return jnp.exp(-(1.0 / r - 1.0 / mu) ** 2 / (2.0 * sigma * sigma))
        key = jax.random.key(seed)
        k_z, k_d, k_w = jax.random.split(key, 3)
        z = jax.random.normal(k_z, (N, D), dtype=jnp.float32)
        dist_matrix = jax.random.uniform(k_d, (N, N), dtype=jnp.float32) * 2.0 + 0.05
        W = jax.random.normal(k_w, (D, D), dtype=jnp.float32)
        B = jnp.zeros((D,), dtype=jnp.float32)
        return {'z': z, 'dist_matrix': dist_matrix, 'W': W, 'B': B}
    _L0_gnn_all = _L0_gnn_setup()
    _L0_gnn_in = {k: v for k, v in _L0_gnn_all.items() if k in ('W', 'B')}
    del _L0_gnn_all

    def _L1_gnn_setup():
        import jax, jax.numpy as jnp
        import numpy as np
        N = 4096
        D_IN = 128
        D_OUT = 128
        key = jax.random.key(seed)
        k1, k2, k3 = jax.random.split(key, 3)
        x = jax.random.normal(k1, (N, D_IN), dtype=jnp.float32)
        adj = jax.random.uniform(k2, (N, N), dtype=jnp.float32)
        W = jax.random.normal(k3, (D_OUT, D_IN), dtype=jnp.float32) * (1.0 / np.sqrt(D_IN))
        return {'x': x, 'adj': adj, 'W': W}
    _L1_gnn_all = _L1_gnn_setup()
    _L1_gnn_in = {k: v for k, v in _L1_gnn_all.items() if k in ('W',)}
    del _L1_gnn_all
    return {'x': x, 'adj': adj, 'L0_gnn_W': _L0_gnn_in['W'], 'L0_gnn_B': _L0_gnn_in['B'], 'L1_gnn_W': _L1_gnn_in['W']}

def reference(x, adj, L0_gnn_W, L0_gnn_B, L1_gnn_W):
    import jax
    import jax.numpy as jnp

    def _L0_gnn_ref(z, dist_matrix, W, B):
        import jax, jax.numpy as jnp
        import numpy as np
        N = 4096
        D = 128
        CUTOFF = 1.0
        MU = 1.0
        SIGMA = 0.5

        def sensitivity(r, mu, sigma):
            return jnp.exp(-(1.0 / r - 1.0 / mu) ** 2 / (2.0 * sigma * sigma))
        msg = z @ W + B
        sens = sensitivity(dist_matrix, MU, SIGMA)
        weights = jnp.where(dist_matrix < CUTOFF, sens, 0.0)
        return weights @ msg

    def _L1_gnn_ref(x, adj, W):
        import jax, jax.numpy as jnp
        import numpy as np
        N = 4096
        D_IN = 128
        D_OUT = 128
        A_hat = adj + jnp.eye(adj.shape[0], dtype=adj.dtype)
        d_inv_sqrt = jnp.sum(A_hat, axis=1) ** (-0.5)
        A_norm = d_inv_sqrt[:, None] * A_hat * d_inv_sqrt[None, :]
        support = x @ W.T
        out = A_norm @ support
        return jax.nn.relu(out)
    h = jnp.maximum(_layernorm(x, axis=-1), 0.0)
    x = x + _L0_gnn_ref(h, adj, L0_gnn_W, L0_gnn_B)
    h = jnp.maximum(_layernorm(x, axis=-1), 0.0)
    x = x + _L1_gnn_ref(h, adj, L1_gnn_W)
    return x

_drawn_inputs = setup_inputs


def setup_inputs(seed=0):
    import zlib

    import numpy as np

    out = dict(_drawn_inputs(seed))
    spreads = {'L0_gnn_B': (0.0, 0.435)}
    factors = {}
    for name, (base, spread) in spreads.items():
        noise = np.random.default_rng([zlib.crc32(name.encode()), seed]).standard_normal(out[name].shape)
        drawn = base * np.exp(spread * noise) if base else spread * noise
        out[name] = jnp.asarray(drawn.astype(out[name].dtype))
    for name, factor in factors.items():
        out[name] = (out[name] * factor).astype(out[name].dtype)
    return out
```

```python
from contextlib import ExitStack

import concourse.bass as bass
from concourse import mybir

P = 128
F32 = mybir.dt.float32
ALU = mybir.AluOpType
ACT = mybir.ActivationFunctionType
AX_X = mybir.AxisListType.X

EPS = 1e-5
CUTOFF = 1.0
LN_GUARD = 2.0 ** -30

MUL_LAG = 2
MIX_LAG = 11


class Step:

    def __init__(self, first, window, groups):
        self.s, self.w, self.g = first, window, groups

    def count(self, n, per=1):
        return n * per + self.w * (self.g * per)

    def group(self, n):
        return n // self.g + self.w


def build(nc, x, adj, w0, b0, w1, out):
    N, D = x.shape
    ROWS = 512
    T = ROWS // P
    G = N // ROWS
    NT = N // P
    NB = G * G
    LAST = NB + MIX_LAG + 2

    ctx = ExitStack()
    with ctx:
        def sb(name, shape):
            return ctx.enter_context(nc.sbuf_tensor(name, shape, F32))

        def ps(name, shape):
            return ctx.enter_context(nc.psum_tensor(name, shape, F32))

        def sem(name):
            return ctx.enter_context(nc.semaphore(name))

        ident = sb("ident", [P, P])
        ones_row = sb("ones_row", [1, P])
        w0_sb = sb("w0_sb", [D, D])
        w1_sb = sb("w1_sb", [D, D])
        w1t = sb("w1t", [D, D])
        b_row = sb("b_row", [1, D])
        b_all = sb("b_all", [P, D])
        x1 = sb("x1", [P, NT, D])
        msg = sb("msg", [P, NT, D])
        support = sb("support", [P, NT, D])
        sup_now = sb("sup_now", [P, T, D])
        mixed = sb("mixed", [D, G, ROWS])
        raw0 = sb("raw0", [P, 2, T, ROWS])
        raw1 = sb("raw1", [P, 2, T, ROWS])
        near = sb("near", [P, 2, T, ROWS])
        wt = sb("wt", [P, 4, T, ROWS])
        adj_t = sb("adj_t", [P, 2, T, ROWS])
        x1t = sb("x1t", [D, ROWS])
        x1_now = sb("x1_now", [P, T, D])
        hid = sb("hid", [P, T, D])
        hid_t = sb("hid_t", [D, 2, ROWS])
        bn = sb("bn", [P, NT, 6])
        mv = sb("mv", [P, NT, 2])
        var0 = sb("var0", [P, NT])
        rs0 = sb("rs0", [P, NT])
        tmp0 = sb("tmp0", [P, NT])
        rowpart = sb("rowpart", [P, T, G])
        pows = sb("pows", [P, 2, T])
        inv = sb("inv", [P, 2, T])
        tmp1 = sb("tmp1", [P, 2, T])
        scale = sb("scale", [P, T])
        dinv = sb("dinv", [P, NT])
        fin = sb("fin", [P, 2, T, D])

        tr0 = ps("tr0", [P, T, ROWS])
        tr1 = ps("tr1", [P, 2, ROWS])
        acc0 = ps("acc0", [D, ROWS])
        acc1 = ps("acc1", [D, ROWS])

        x_loaded = sem("x_loaded")
        w_loaded = sem("w_loaded")
        raw0_loaded = [sem("raw0_loaded0"), sem("raw0_loaded1")]
        raw1_loaded = [sem("raw1_loaded0"), sem("raw1_loaded1")]
        out_written = [sem("out_written0"), sem("out_written1")]
        zeroed = sem("zeroed")
        ident_zeroed = sem("ident_zeroed")
        ident_done = sem("ident_done")
        near_done = sem("near_done")
        summed = sem("summed")
        tr0_done = sem("tr0_done")
        tr1_done = sem("tr1_done")
        ln_done = sem("ln_done")
        inv_done = sem("inv_done")
        quad_done = sem("quad_done")
        wt_done = sem("wt_done")
        adj_t_done = sem("adj_t_done")
        acc0_done = sem("acc0_done")
        acc1_done = sem("acc1_done")
        added = sem("added")
        rows_summed = sem("rows_summed")
        x1t_copied = sem("x1t_copied")
        x1_turned = sem("x1_turned")
        x1_done = sem("x1_done")
        x1_kept = sem("x1_kept")
        stats_done = sem("stats_done")
        moments_done = sem("moments_done")
        pows_done = sem("pows_done")
        pows_ln = sem("pows_ln")
        pows_exp = sem("pows_exp")
        newton = sem("newton")
        dinv_done = sem("dinv_done")
        scale_done = sem("scale_done")
        hid_done = sem("hid_done")
        hid_turned = sem("hid_turned")
        hid_t_done = sem("hid_t_done")
        sup_multiplied = sem("sup_multiplied")
        sup_done = sem("sup_done")
        sup_ready = sem("sup_ready")
        bn_all = sem("bn_all")
        mv_all = sem("mv_all")
        var_all = sem("var_all")
        ln_all = sem("ln_all")
        exp_all = sem("exp_all")
        newton_all = sem("newton_all")
        h0_done = sem("h0_done")
        h0_turned = sem("h0_turned")
        h0_t_done = sem("h0_t_done")
        m_multiplied = sem("m_multiplied")
        msg_done = sem("msg_done")
        small_mm = sem("small_mm")
        small_copied = sem("small_copied")
        mix_turned = sem("mix_turned")
        out_summed = sem("out_summed")
        out_relu = sem("out_relu")
        out_done = sem("out_done")

        adj_blocks = adj.rearrange("(g a p) (c j) -> g c p a j", a=T, p=P, j=ROWS)
        x_rows = x.rearrange("(t p) d -> p t d", p=P)
        out_rows = out.rearrange("(g a p) d -> g p a d", a=T, p=P)

        FIRST = MIX_LAG + 2
        WINDOWS = (NB - FIRST) // G

        def run(eng, body):
            for s in range(FIRST):
                body(Step(s, 0, G))
            with eng.Fori(0, WINDOWS) as w:
                for s in range(FIRST, FIRST + G):
                    body(Step(s, w, G))
            for s in range(FIRST + G * WINDOWS, LAST):
                body(Step(s, 0, G))

        block = ctx.enter_context(nc.Block())

        @block.sync
        def _(sp):
            def load_weigh(t, n):
                if n >= 2:
                    sp.wait_ge(summed, t.count(n - 1))
                sp.dma_start(raw0[:, n % 2], adj_blocks[t.group(n), n % G]).then_inc(raw0_loaded[n % 2], 16)

            def load_mix(t, m):
                if m >= 2:
                    sp.wait_ge(tr1_done, t.count(m - 1, T))
                sp.dma_start(raw1[:, m % 2], adj_blocks[m % G, t.group(m)]).then_inc(raw1_loaded[m % 2], 16)

            def step(t):
                if t.s + 2 < NB:
                    load_weigh(t, t.s + 2)
                m = t.s - MIX_LAG + 1
                if 0 <= m < NB:
                    load_mix(t, m)

            sp.dma_start(x1[:], x_rows).then_inc(x_loaded, 16)
            load_weigh(Step(0, 0, G), 0)
            sp.dma_start(w0_sb[:], w0).then_inc(w_loaded, 16)
            sp.dma_start(w1_sb[:], w1).then_inc(w_loaded, 16)
            sp.dma_start(b_row[:], b0.rearrange("(a d) -> a d", a=1)).then_inc(w_loaded, 16)
            load_weigh(Step(1, 0, G), 1)
            run(sp, step)
            for k in range(G):
                sp.wait_ge(out_done, k + 1)
                sp.dma_start(out_rows[k], fin[:, k % 2]).then_inc(out_written[k % 2], 16)
            for b in range(2):
                sp.wait_ge(out_written[b], 16 * (G // 2))

        @block.gpsimd
        def _(pool):
            nc.gpsimd.memset(ident[:], 0.0).then_inc(ident_zeroed, 1)
            nc.gpsimd.memset(ones_row[:], 1.0)
            pool.wait_ge(ident_zeroed, 1)
            nc.gpsimd.affine_select(out=ident[:], in_=ident[:], compare_op=ALU.not_equal, fill=1.0, base=0,
                                    pattern=[[-1, P]], channel_multiplier=1).then_inc(ident_done, 1)
            nc.gpsimd.memset(mixed[:], 0.0).then_inc(zeroed, 1)

            def keep_x1(g):
                pool.wait_ge(x1_done, g + 1)
                nc.gpsimd.tensor_copy(x1[:, bass.ds(g * T, T), :], x1_now[:]).then_inc(x1_kept, 1)

            def copy_support(g):
                pool.wait_ge(sup_done, g + 1)
                pool.wait_ge(acc1_done, g * G)
                nc.gpsimd.tensor_copy(sup_now[:], support[:, bass.ds(g * T, T), :]).then_inc(sup_ready, 1)

            keep_x1(0)
            pool.wait_ge(sup_done, 1)
            nc.gpsimd.tensor_copy(sup_now[:], support[:, 0:T, :]).then_inc(sup_ready, 1)
            with pool.Fori(1, G) as g:
                keep_x1(g)
                copy_support(g)

        @block.tensor
        def _(pe):
            def turn_weigh(t, n, q):
                if q == 0:
                    pe.wait_ge(near_done, t.count(n + 1))
                if q % 2 == 0 and n >= 1:
                    pe.wait_ge(ln_done, t.count(n - 1, 2) + q // 2 + 1)
                for a in range(T):
                    last = nc.tensor.transpose(tr0[:, q, a * P:(a + 1) * P], near[:, n % 2, a, q * P:(q + 1) * P],
                                               ident[:])
                if q % 2 == 1:
                    last.then_inc(tr0_done, 1)

            def turn_mix(t, m, q, bank, freed=1):
                if q == 0:
                    pe.wait_ge(raw1_loaded[m % 2], (m // 2 + 1) * 16 + t.w * (16 * G // 2))
                if 4 * m + q - freed >= 0:
                    pe.wait_ge(adj_t_done, t.count(m, T) + q - freed)
                for a in range(T):
                    last = nc.tensor.transpose(tr1[:, bank, a * P:(a + 1) * P], raw1[:, m % 2, a, q * P:(q + 1) * P],
                                               ident[:])
                last.then_inc(tr1_done, 1)

            def multiply_weigh(t, n, q):
                c = n % G
                if q == 0:
                    pe.wait_ge(wt_done, t.count(n + 1))
                    if n >= G and c == 0:
                        pe.wait_ge(x1t_copied, t.group(n))
                mm = nc.tensor.matmul(acc0[:], msg[:, c * T + q, :], wt[:, n % 4, q, :],
                                      start=(c == 0 and q == 0), stop=(c == G - 1 and q == T - 1))
                if q == T - 1:
                    mm.then_inc(acc0_done, 1)

            def multiply_mix(t, m, q):
                if q == 0:
                    pe.wait_ge(adj_t_done, t.count(m + 1, T))
                    if m >= 1:
                        pe.wait_ge(added, t.count(m))
                    if m % G == 0:
                        pe.wait_ge(sup_ready, t.group(m) + 1)
                mm = nc.tensor.matmul(acc1[:], sup_now[:, q, :], adj_t[:, m % 2, q, :],
                                      start=(q == 0), stop=(q == T - 1))
                if q == T - 1:
                    mm.then_inc(acc1_done, 1)

            def turn_x1(t, g, bank):
                pe.wait_ge(x1t_copied, t.group(g * G) + 1)
                for a in range(T):
                    last = nc.tensor.transpose(tr1[:, bank, a * P:(a + 1) * P], x1t[:, a * P:(a + 1) * P], ident[:])
                last.then_inc(x1_turned, 1)

            def turn_hid(t, g, bank):
                pe.wait_ge(hid_done, t.group(g * G) + 1)
                for a in range(T):
                    last = nc.tensor.transpose(tr1[:, bank, a * P:(a + 1) * P], hid[:, a, :], ident[:])
                last.then_inc(hid_turned, 1)

            def multiply_support(t, g, bank):
                pe.wait_ge(hid_t_done, t.group(g * G) + 1)
                for a in range(T):
                    mm = nc.tensor.matmul(tr1[:, bank, a * P:(a + 1) * P], hid_t[:, 0, a * P:(a + 1) * P], w1t[:],
                                          start=True, stop=True)
                mm.then_inc(sup_multiplied, 1)

            def turn_out(k):
                pe.wait_ge(added, NB - G + k + 1)
                if k >= 2:
                    pe.wait_ge(out_summed, k - 1)
                else:
                    pe.wait_ge(ln_done, 2 * NB)
                for a in range(T):
                    last = nc.tensor.transpose(tr0[:, k % 2, a * P:(a + 1) * P], mixed[:, k, a * P:(a + 1) * P],
                                               ident[:])
                last.then_inc(mix_turned, 1)

            def step(t):
                s = t.s
                weigh, weigh_mul = s < NB, MUL_LAG <= s < NB + MUL_LAG
                m = s - MIX_LAG
                mix, mix_mul = 0 <= m < NB, 1 <= m < NB + 1
                g = (s - G) // G
                ended, follows = 0 <= g < G and s % G == 2, 0 <= g < G and s % G == 3
                for q in range(T):
                    if weigh:
                        turn_weigh(t, s, q)
                    if ended:
                        if mix:
                            if q == 2:
                                pe.wait_ge(x1_done, t.group(g * G) + 1)
                            turn_mix(t, m, q, [0, 0, 1, 1][q], freed=[1, 0, 1, 0][q])
                        if q == 0:
                            if mix and m >= 1:
                                pe.wait_ge(adj_t_done, t.count(m, T))
                            turn_x1(t, g, 1)
                        if q == 2:
                            if mix:
                                pe.wait_ge(adj_t_done, t.count(m, T) + 2)
                            turn_hid(t, g, 0)
                    elif follows:
                        if mix:
                            if q == 0:
                                pe.wait_ge(hid_t_done, t.group(g * G) + 1)
                            if q == 2:
                                pe.wait_ge(sup_done, t.group(g * G) + 1)
                            turn_mix(t, m, q, [0, 0, 1, 0][q], freed=[1, 0, 1, 1][q])
                        if q == 0:
                            if mix and m >= 1:
                                pe.wait_ge(adj_t_done, t.count(m, T))
                            multiply_support(t, g, 1)
                    elif mix:
                        turn_mix(t, m, q, q % 2, freed=0 if q == 0 else 1)
                    if weigh_mul and q in (0, 3):
                        multiply_weigh(t, s - MUL_LAG, 0 if q == 0 else 2)
                        multiply_weigh(t, s - MUL_LAG, 1 if q == 0 else 3)
                    if mix_mul and q in (1, 2):
                        multiply_mix(t, m - 1, 0 if q == 1 else 2)
                        multiply_mix(t, m - 1, 1 if q == 1 else 3)
                if t.s >= LAST - G and isinstance(t.w, int):
                    turn_out(t.s - (LAST - G))

            pe.wait_ge(ident_done, 1)
            pe.wait_ge(w_loaded, 48)
            nc.tensor.matmul(tr1[:, 0, 0:D], ones_row[:], b_row[:], start=True, stop=True)
            nc.tensor.transpose(tr1[:, 1, 0:D], w1_sb[:], ident[:]).then_inc(small_mm, 1)
            pe.wait_ge(small_copied, 1)
            for g in range(G):
                pe.wait_ge(h0_done, g + 1)
                if g >= 2:
                    pe.wait_ge(h0_t_done, g - 1)
                for a in range(T):
                    last = nc.tensor.transpose(tr1[:, g % 2, a * P:(a + 1) * P], support[:, g * T + a, :], ident[:])
                last.then_inc(h0_turned, 1)
                pe.wait_ge(h0_t_done, g + 1)
                if g >= 2:
                    pe.wait_ge(msg_done, g - 1)
                bank = (acc0, acc1)[g % 2]
                for a in range(T):
                    last = nc.tensor.matmul(bank[:, a * P:(a + 1) * P], hid_t[:, g % 2, a * P:(a + 1) * P], w0_sb[:],
                                            start=True, stop=True)
                last.then_inc(m_multiplied, 1)
            pe.wait_ge(msg_done, G)
            run(pe, step)

        @block.scalar
        def _(act):
            def log(t, n, half):
                act.wait_ge(tr0_done, t.count(n, 2) + half + 1)
                if half == 0 and n >= 4:
                    act.wait_ge(acc0_done, t.count(n - 3))
                q = half * 2
                nc.scalar.activation(wt[:, n % 4, q:q + 2, :], tr0[:, q:q + 2, :], ACT.Ln,
                                     bias=LN_GUARD).then_inc(ln_done, 1)

            def invert(t, n):
                act.wait_ge(ln_done, t.count(n + 1, 2))
                nc.scalar.activation(wt[:, n % 4], wt[:, n % 4], ACT.Exp, scale=-1.0).then_inc(inv_done, 1)

            def weigh(t, n):
                act.wait_ge(quad_done, t.count(n + 1))
                nc.scalar.activation(wt[:, n % 4], wt[:, n % 4], ACT.Exp, scale=-2.0, bias=-2.0).then_inc(wt_done, 1)

            def copy_mix(t, m, q, bank):
                act.wait_ge(tr1_done, t.count(m, T) + q + 1)
                if q == 0 and m >= 2:
                    act.wait_ge(acc1_done, t.count(m - 1))
                nc.scalar.copy(adj_t[:, m % 2, q, :], tr1[:, bank, :]).then_inc(adj_t_done, 1)

            def step(t):
                s = t.s
                m = s - MIX_LAG
                g = (s - G) // G
                ended, follows = 0 <= g < G and s % G == 2, 0 <= g < G and s % G == 3
                banks = [0, 0, 1, 1] if ended else [0, 0, 1, 0] if follows else [0, 1, 0, 1]
                mix = 0 <= m < NB
                if mix:
                    copy_mix(t, m, 0, banks[0])
                if s < NB:
                    log(t, s, 0)
                if mix:
                    copy_mix(t, m, 1, banks[1])
                if 1 <= s < NB + 1:
                    weigh(t, s - 1)
                if mix:
                    copy_mix(t, m, 2, banks[2])
                if ended:
                    act.wait_ge(hid_turned, t.group(g * G) + 1)
                    nc.scalar.copy(hid_t[:, 0, :], tr1[:, 0, :]).then_inc(hid_t_done, 1)
                    act.wait_ge(pows_done, t.group(g * G) + 1)
                    nc.scalar.activation(inv[:], pows[:], ACT.Ln).then_inc(pows_ln, 1)
                    act.wait_ge(pows_ln, t.group(g * G) + 1)
                    nc.scalar.activation(inv[:], inv[:], ACT.Exp, scale=-0.5).then_inc(pows_exp, 1)
                if s < NB:
                    log(t, s, 1)
                if mix:
                    copy_mix(t, m, 3, banks[3])
                if s < NB:
                    invert(t, s)

            act.wait_ge(small_mm, 1)
            nc.scalar.copy(w1t[:], tr1[:, 1, 0:D])
            nc.scalar.copy(b_all[:], tr1[:, 0, 0:D]).then_inc(small_copied, 1)
            act.wait_ge(var_all, 1)
            nc.scalar.activation(rs0[:], var0[:], ACT.Ln).then_inc(ln_all, 1)
            act.wait_ge(ln_all, 1)
            nc.scalar.activation(rs0[:], rs0[:], ACT.Exp, scale=-0.5).then_inc(exp_all, 1)
            for g in range(G):
                act.wait_ge(h0_turned, g + 1)
                if g >= 2:
                    act.wait_ge(m_multiplied, g - 1)
                nc.scalar.copy(hid_t[:, g % 2, :], tr1[:, g % 2, :]).then_inc(h0_t_done, 1)
            run(act, step)

        @block.vector
        def _(dve):
            def cut(t, n):
                dve.wait_ge(raw0_loaded[n % 2], (n // 2 + 1) * 16 + t.w * (16 * G // 2))
                if n >= 2:
                    dve.wait_ge(tr0_done, t.count(n - 1, 2))
                nc.vector.scalar_tensor_tensor(out=near[:, n % 2], in0=raw0[:, n % 2], scalar=CUTOFF,
                                               in1=raw0[:, n % 2], op0=ALU.is_lt, op1=ALU.mult).then_inc(near_done, 1)

            def row_sum(t, n):
                c = n % G
                if c == 0 and n >= G:
                    dve.wait_ge(rows_summed, t.group(n))
                nc.vector.tensor_reduce(rowpart[:, :, c:c + 1], raw0[:, n % 2], AX_X, ALU.add).then_inc(summed, 1)
                if c == G - 1:
                    dve.wait_ge(summed, t.count(n + 1))
                    if n >= G:
                        dve.wait_ge(pows_ln, t.group(n))
                    nc.vector.tensor_reduce(pows[:, 0, :], rowpart[:], AX_X, ALU.add).then_inc(rows_summed, 1)

            def quad(t, n):
                dve.wait_ge(inv_done, t.count(n + 1))
                v = wt[:, n % 4]
                nc.vector.scalar_tensor_tensor(out=v, in0=v, scalar=-2.0, in1=v, op0=ALU.add,
                                               op1=ALU.mult).then_inc(quad_done, 1)

            def add_mix(t, m):
                k = m % G
                dve.wait_ge(acc1_done, t.count(m + 1))
                if m >= 1:
                    dve.wait_ge(added, t.count(m))
                nc.vector.tensor_tensor(mixed[:, k, :], acc1[:], mixed[:, k, :], ALU.add).then_inc(added, 1)

            def end_rows(t, g):
                n = t.group(g * G)
                dve.wait_ge(acc0_done, t.count((g + 1) * G))
                if g >= 1:
                    dve.wait_ge(x1_turned, n)
                nc.vector.tensor_copy(x1t[:], acc0[:]).then_inc(x1t_copied, 1)
                if 1 <= t.s < NB + 1:
                    quad(t, t.s - 1)
                dve.wait_ge(x1_turned, n + 1)
                if g >= 1:
                    dve.wait_ge(x1_kept, n)
                nc.vector.tensor_tensor(x1_now[:], tr1[:, 1, :].rearrange("p (a d) -> p a d", a=T),
                                        x1[:, bass.ds(n * T, T), :], ALU.add).then_inc(x1_done, 1)
                dve.wait_ge(x1_done, n + 1)
                for a in range(T):
                    last = nc.vector.bn_stats(bn[:, a, :], x1_now[:, a, :])
                last.then_inc(stats_done, 1)
                dve.wait_ge(rows_summed, n + 1)
                dve.wait_ge(stats_done, n + 1)
                nc.vector.tensor_scalar(pows[:, 0, :], pows[:, 0, :], 1.0, None, ALU.add)
                for a in range(T):
                    last = nc.vector.bn_aggr(mv[:, a, :], bn[:, a, :])
                last.then_inc(moments_done, 1)
                dve.wait_ge(moments_done, n + 1)
                if g >= 1:
                    dve.wait_ge(hid_turned, n)
                for a in range(T):
                    last = nc.vector.tensor_scalar(hid[:, a, :], x1_now[:, a, :], mv[:, a, 0:1], 0.0,
                                                   ALU.subtract, ALU.max)
                last.then_inc(hid_done, 1)
                nc.vector.tensor_scalar(pows[:, 1, :], mv[:, 0:T, 1], EPS, None, ALU.add).then_inc(pows_done, 1)

            def newton_step(y, a, tmp, done, before):
                nc.vector.tensor_tensor(tmp, y, y, ALU.mult).then_inc(done, 1)
                dve.wait_ge(done, before + 1)
                nc.vector.scalar_tensor_tensor(out=tmp, in0=tmp, scalar=-0.5, in1=a, op0=ALU.mult,
                                               op1=ALU.mult).then_inc(done, 1)
                dve.wait_ge(done, before + 2)
                nc.vector.scalar_tensor_tensor(out=y, in0=tmp, scalar=1.5, in1=y, op0=ALU.add,
                                               op1=ALU.mult).then_inc(done, 1)
                dve.wait_ge(done, before + 3)

            def make_support(t, g):
                n = t.group(g * G)
                dve.wait_ge(pows_exp, n + 1)
                newton_step(inv[:], pows[:], tmp1[:], newton, n * 3)
                nc.vector.tensor_copy(dinv[:, bass.ds(n * T, T)], inv[:, 0, :]).then_inc(dinv_done, 1)
                nc.vector.tensor_tensor(scale[:], inv[:, 0, :], inv[:, 1, :], ALU.mult).then_inc(scale_done, 1)
                dve.wait_ge(scale_done, n + 1)
                dve.wait_ge(sup_multiplied, n + 1)
                for a in range(T):
                    last = nc.vector.tensor_scalar(support[:, bass.ds(n * T + a, 1), :], tr1[:, 1, a * P:(a + 1) * P],
                                                   scale[:, a:a + 1], None, ALU.mult)
                last.then_inc(sup_done, 1)

            def finish(k):
                if k == 0:
                    dve.wait_ge(x1_kept, G)
                dve.wait_ge(mix_turned, k + 1)
                if k >= 2:
                    dve.wait_ge(out_written[k % 2], 16 * (k // 2))
                rows = slice(k * T, k * T + T)
                nc.vector.tensor_tensor(fin[:, k % 2], tr0[:, k % 2, :].rearrange("p (a d) -> p a d", a=T),
                                        support[:, rows, :], ALU.add).then_inc(out_summed, 1)
                dve.wait_ge(out_summed, k + 1)
                for a in range(T):
                    last = nc.vector.tensor_scalar(fin[:, k % 2, a, :], fin[:, k % 2, a, :],
                                                   dinv[:, k * T + a:k * T + a + 1], 0.0, ALU.mult, ALU.max)
                last.then_inc(out_relu, 1)
                dve.wait_ge(out_relu, k + 1)
                nc.vector.tensor_tensor(fin[:, k % 2], fin[:, k % 2], x1[:, rows, :], ALU.add).then_inc(out_done, 1)

            def step(t):
                s = t.s
                g = (s - G) // G
                ended, follows = 0 <= g < G and s % G == 2, 0 <= g < G and s % G == 3
                if ended:
                    end_rows(t, g)
                elif 1 <= s < NB + 1:
                    quad(t, s - 1)
                if follows:
                    make_support(t, g)
                if s + 1 < NB:
                    cut(t, s + 1)
                    row_sum(t, s + 1)
                m = s - MIX_LAG - 1
                if 0 <= m < NB:
                    add_mix(t, m)
                if t.s >= LAST - G and isinstance(t.w, int):
                    finish(t.s - (LAST - G))

            cut(Step(0, 0, G), 0)
            row_sum(Step(0, 0, G), 0)
            dve.wait_ge(x_loaded, 16)
            for a in range(NT):
                last = nc.vector.bn_stats(bn[:, a, :], x1[:, a, :])
            last.then_inc(bn_all, 1)
            dve.wait_ge(bn_all, 1)
            for a in range(NT):
                last = nc.vector.bn_aggr(mv[:, a, :], bn[:, a, :])
            last.then_inc(mv_all, 1)
            dve.wait_ge(mv_all, 1)
            nc.vector.tensor_scalar(var0[:], mv[:, :, 1], EPS, None, ALU.add).then_inc(var_all, 1)
            for g in range(G):
                for a in range(g * T, g * T + T):
                    last = nc.vector.tensor_scalar(support[:, a, :], x1[:, a, :], mv[:, a, 0:1], 0.0,
                                                   ALU.subtract, ALU.max)
                last.then_inc(h0_done, 1)
            dve.wait_ge(exp_all, 1)
            newton_step(rs0[:], var0[:], tmp0[:], newton_all, 0)
            dve.wait_ge(small_copied, 1)
            for g in range(G):
                dve.wait_ge(m_multiplied, g + 1)
                bank = (acc0, acc1)[g % 2]
                for a in range(T):
                    n = g * T + a
                    last = nc.vector.scalar_tensor_tensor(out=msg[:, n, :], in0=bank[:, a * P:(a + 1) * P],
                                                          scalar=rs0[:, n:n + 1], in1=b_all[:], op0=ALU.mult,
                                                          op1=ALU.add)
                last.then_inc(msg_done, 1)
            dve.wait_ge(zeroed, 1)
            run(dve, step)


_INS = ["x", "adj", "L0_gnn_W", "L0_gnn_B", "L1_gnn_W"]


def kernel(**inputs):
    import numpy as _np
    import concourse.bacc as _bacc
    from concourse import mybir as _mybir
    from concourse.bass_utils import run_bass_kernel_spmd as _run

    nc = _bacc.Bacc("TRN2", target_bir_lowering=False, num_devices=1)
    arrays, args = {}, []
    for name in _INS:
        a = _np.ascontiguousarray(inputs[name])
        arrays[f"in_{name}_dram"] = a
        args.append(nc.dram_tensor(f"in_{name}_dram", a.shape, _mybir.dt.from_np(a.dtype), kind="ExternalInput").ap())
    shape = inputs["x"].shape
    args.append(nc.dram_tensor("out_0_dram", shape, _mybir.dt.float32, kind="ExternalOutput").ap())
    build(nc, *args)
    r = _run(nc, [arrays], core_ids=[0])
    return r.results[0]["out_0_dram"]
```

```python
from contextlib import ExitStack

import concourse.bass as bass
from concourse import mybir

P = 128
F32 = mybir.dt.float32
ALU = mybir.AluOpType
ACT = mybir.ActivationFunctionType
AX_X = mybir.AxisListType.X

EPS = 1e-5
CUTOFF = 1.0
LN_GUARD = 2.0 ** -30

G = 8
ORDER = [0, 1, 3, 4, 7, 2, 5, 6]
PHASES = [(0, 1, 0), (1, 2, 0), (3, 3, 3), (6, 2, 6)]
LATE = {
    0: [],
    3: [(3, 0, 0, True, False, 0), (4, 0, 1, False, False, 0), (5, 0, 2, False, True, 0)],
    6: [(1, 0, 3, True, False, 0), (2, 0, 4, False, True, 0), (3, 1, 3, True, False, 0), (4, 1, 4, False, True, 0),
        (5, 2, 3, True, False, 0), (5, 2, 4, False, True, 0), (6, 0, 5, True, True, 0), (7, 1, 5, True, True, 1),
        (7, 2, 5, True, True, 0)],
}
SHARE = {0: 0, 3: 1, 6: 3}
ADDS = {
    0: [],
    3: [(6, 0, 0), (7, "once", None)],
    6: [(3, 0, 0), (5, 1, 0), (6, 2, 0), (7, 0, 0), (G, "once", None), (G, 1, 1), (G, 2, 0)],
}
LATE_SLOTS = 3
RAW, KEPT, WTS = 4, 4, 4
AHEAD = 3
MUL_LAG = 3


def stored(known, slot=None):
    return [int(c >= known and slot in (None, p % KEPT)) for p, c in enumerate(ORDER)]


def at_once(known):
    return [int(c < known) for c in ORDER]


def per_step(items, known):
    return [sum(min(i[0], G - 1) == p for i in items[known]) for p in range(G)]


class Turn:

    def __init__(self, first, w, known):
        self.first, self.w, self.known = first, w, known
        self.row = first + w

    def blocks(self, p, per=1):
        return (self.first * G + p) * per + self.w * (G * per)

    def tally(self, events, p=0):
        before = sum(sum(events(k)) * n for f, n, k in PHASES if f < self.first)
        return before + self.w * sum(events(self.known)) + sum(events(self.known)[:p])


def build(nc, x, adj, w0, b0, w1, out):
    N, D = x.shape
    ROWS = N // G
    T = ROWS // P
    NT = N // P
    NB = G * G

    ctx = ExitStack()
    with ctx:
        def sb(name, shape):
            return ctx.enter_context(nc.sbuf_tensor(name, shape, F32))

        def ps(name, shape):
            return ctx.enter_context(nc.psum_tensor(name, shape, F32))

        def sem(name):
            return ctx.enter_context(nc.semaphore(name))

        spill = nc.dram_tensor("adj_t_spill", [G, G + 1, P, T, ROWS], F32, kind="Internal").ap()

        ident = sb("ident", [P, P])
        ones_row = sb("ones_row", [1, P])
        w0_sb = sb("w0_sb", [D, D])
        w1_sb = sb("w1_sb", [D, D])
        w1t = sb("w1t", [D, D])
        b_row = sb("b_row", [1, D])
        b_all = sb("b_all", [P, D])
        x1 = sb("x1", [P, NT, D])
        msg = sb("msg", [P, NT, D])
        support = sb("support", [P, NT, D])
        mixed = sb("mixed", [D, G, ROWS])
        raw = sb("raw", [P, RAW, T, ROWS])
        kept = sb("kept", [P, KEPT, T, ROWS])
        late = sb("late", [P, LATE_SLOTS, T, ROWS])
        wt = sb("wt", [P, WTS, T, ROWS])
        x1t = sb("x1t", [D, ROWS])
        x1_now = sb("x1_now", [P, T, D])
        hid = sb("hid", [P, T, D])
        hid_t = sb("hid_t", [D, ROWS])
        bn = sb("bn", [P, NT, 6])
        mv = sb("mv", [P, NT, 2])
        var0 = sb("var0", [P, NT])
        rs0 = sb("rs0", [P, NT])
        tmp0 = sb("tmp0", [P, NT])
        rowpart = sb("rowpart", [P, T, G])
        pows = sb("pows", [P, 2, T])
        inv = sb("inv", [P, 2, T])
        tmp1 = sb("tmp1", [P, 2, T])
        scale = sb("scale", [P, T])
        dinv = sb("dinv", [P, NT])
        mix_end = sb("mix_end", [D, 2, ROWS])
        fin = sb("fin", [P, 2, T, D])

        turned_ps = ps("turned_ps", [P, T, ROWS])
        acc0 = ps("acc0", [D, ROWS])
        acc_once = ps("acc_once", [D, ROWS])
        acc_late = ps("acc_late", [D, ROWS])
        side = ps("side", [P, ROWS])

        x_loaded = sem("x_loaded")
        w_loaded = sem("w_loaded")
        raw_loaded = [sem(f"raw_loaded{i}") for i in range(RAW)]
        spilled = [sem(f"spilled{i}") for i in range(KEPT)]
        late_loaded = [sem(f"late_loaded{i}") for i in range(LATE_SLOTS)]
        out_written = [sem(f"out_written{i}") for i in range(2)]
        ident_zeroed = sem("ident_zeroed")
        ident_done = sem("ident_done")
        turned = sem("turned")
        copied = sem("copied")
        summed = sem("summed")
        cut_done = sem("cut_done")
        ln_done = sem("ln_done")
        inv_done = sem("inv_done")
        quad_done = sem("quad_done")
        wt_done = sem("wt_done")
        acc0_done = sem("acc0_done")
        once_done = sem("once_done")
        late_done = sem("late_done")
        added = sem("added")
        x1_kept = sem("x1_kept")
        rows_summed = sem("rows_summed")
        x1t_copied = sem("x1t_copied")
        x1_turned = sem("x1_turned")
        x1_done = sem("x1_done")
        stats_done = sem("stats_done")
        moments_done = sem("moments_done")
        pows_done = sem("pows_done")
        pows_ln = sem("pows_ln")
        pows_exp = sem("pows_exp")
        newton = sem("newton")
        dinv_done = sem("dinv_done")
        scale_done = sem("scale_done")
        hid_done = sem("hid_done")
        hid_turned = sem("hid_turned")
        hid_t_done = sem("hid_t_done")
        sup_multiplied = sem("sup_multiplied")
        sup_done = sem("sup_done")
        small_mm = sem("small_mm")
        small_copied = sem("small_copied")
        bn_all = sem("bn_all")
        mv_all = sem("mv_all")
        var_all = sem("var_all")
        ln_all = sem("ln_all")
        exp_all = sem("exp_all")
        newton_all = sem("newton_all")
        h0_done = sem("h0_done")
        h0_turned = sem("h0_turned")
        h0_t_done = sem("h0_t_done")
        m_multiplied = sem("m_multiplied")
        msg_done = sem("msg_done")
        end_mixed = sem("end_mixed")
        end_added = sem("end_added")
        mix_turned = sem("mix_turned")
        out_summed = sem("out_summed")
        out_relu = sem("out_relu")
        out_done = sem("out_done")

        adj_blocks = adj.rearrange("(g a p) (c j) -> g c p a j", a=T, p=P, j=ROWS)
        x_rows = x.rearrange("(t p) d -> p t d", p=P)
        out_rows = out.rearrange("(g a p) d -> g p a d", a=T, p=P)

        NUM_ADDS = sum(n * len(ADDS[k]) for _, n, k in PHASES)
        NUM_LATE = sum(n * len(LATE[k]) for _, n, k in PHASES)
        LAST_KNOWN = PHASES[-1][2]
        END = [(r, c) for rows in (range(T), range(T, G)) for c in range(LAST_KNOWN, G) for r in rows]

        def turns(eng, turn, phases):
            for first, n, known in phases:
                if n == 1:
                    turn(Turn(first, 0, known))
                else:
                    with eng.Fori(0, n) as w:
                        turn(Turn(first, w, known))

        block = ctx.enter_context(nc.Block())

        @block.sync
        def _(sp):
            def load(t, p, n):
                if n >= RAW:
                    sp.wait_ge(cut_done, t.blocks(p - RAW + 1))
                sp.dma_start(raw[:, p % RAW], adj_blocks[t.row + p // G, ORDER[p % G]]).then_inc(raw_loaded[p % RAW], 16)

            def store(t, p):
                sp.wait_ge(copied, t.blocks(p + 1, 2))
                sp.dma_start(spill[t.row, 1 + ORDER[p]], kept[:, p % KEPT]).then_inc(spilled[p % KEPT], 16)

            def load_late(t, j):
                _, r, c, _, _, _ = LATE[t.known][j]
                jobs = t.tally(lambda k: per_step(LATE, k)) + j
                freed = jobs - LATE_SLOTS + 2 if j >= LATE_SLOTS else t.tally(lambda k: per_step(LATE, k)) + 1
                sp.wait_ge(late_done, freed)
                sp.dma_start(late[:, j % LATE_SLOTS], spill[t.w * SHARE[t.known] + r, 1 + c]).then_inc(late_loaded[j % LATE_SLOTS], 16)

            def wait_spilled(first):
                for slot in range(KEPT):
                    sp.wait_ge(spilled[slot], 16 * sum(n * sum(stored(k, slot)) for f, n, k in PHASES if f < first))

            def turn(t, last=False):
                jobs = LATE[t.known]
                for p in range(G):
                    if not (last and p + AHEAD >= G):
                        load(t, p + AHEAD, t.first * G + p + AHEAD)
                    if stored(t.known)[p]:
                        store(t, p)
                    for j, job in enumerate(jobs):
                        if job[0] == p + 1:
                            load_late(t, j)

            sp.dma_start(x1[:, 0:NT // 2], x_rows[:, 0:NT // 2]).then_inc(x_loaded, 16)
            sp.dma_start(x1[:, NT // 2:NT], x_rows[:, NT // 2:NT]).then_inc(x_loaded, 16)
            first = Turn(0, 0, 0)
            load(first, 0, 0)
            sp.dma_start(w0_sb[:], w0).then_inc(w_loaded, 16)
            sp.dma_start(w1_sb[:], w1).then_inc(w_loaded, 16)
            sp.dma_start(b_row[:], b0.rearrange("(a d) -> a d", a=1)).then_inc(w_loaded, 16)
            for n in range(1, AHEAD):
                load(first, n, n)
            for phase in PHASES[:-1]:
                wait_spilled(phase[0])
                turns(sp, turn, [phase])
            f, n, known = PHASES[-1]
            wait_spilled(f)
            turn(Turn(f, 0, known))
            turn(Turn(f, 1, known), last=True)
            wait_spilled(G)
            for j, (r, c) in enumerate(END):
                sp.wait_ge(late_done, NUM_LATE + j - LATE_SLOTS + 2)
                slot = (NUM_LATE + j) % LATE_SLOTS
                sp.dma_start(late[:, slot], spill[r, 1 + c]).then_inc(late_loaded[slot], 16)
            for r in range(G):
                sp.wait_ge(out_done, r + 1)
                sp.dma_start(out_rows[r], fin[:, r % 2]).then_inc(out_written[r % 2], 16)
            for b in range(2):
                sp.wait_ge(out_written[b], 16 * (G // 2))

        @block.gpsimd
        def _(pool):
            nc.gpsimd.memset(ident[:], 0.0).then_inc(ident_zeroed, 1)
            nc.gpsimd.memset(ones_row[:], 1.0).then_inc(x1_kept, 1)
            pool.wait_ge(ident_zeroed, 1)
            nc.gpsimd.affine_select(out=ident[:], in_=ident[:], compare_op=ALU.not_equal, fill=1.0, base=0,
                                    pattern=[[-1, P]], channel_multiplier=1).then_inc(ident_done, 1)
            nc.gpsimd.memset(mixed[:, 0:G // 2], 0.0).then_inc(once_done, 1)
            nc.gpsimd.memset(mixed[:, G // 2:G - 1], 0.0).then_inc(late_done, 1)
            nc.gpsimd.memset(mixed[:, G - 1:G], 0.0).then_inc(added, 1)
            with pool.Fori(0, G) as g:
                pool.wait_ge(x1_done, g + 1)
                nc.gpsimd.tensor_copy(x1[:, bass.ds(g * T, T), :], x1_now[:]).then_inc(x1_kept, 1)

        @block.tensor
        def _(pe):
            def turn_tile(t, p, q):
                n = t.first * G + p
                if q == 0:
                    pe.wait_ge(raw_loaded[p % RAW], (n // RAW + 1) * 16 + t.w * (16 * G // RAW))
                if q % 2 == 0 and n >= 1:
                    pe.wait_ge(copied, t.blocks(p - 1, 2) + q // 2 + 1)
                for a in range(T):
                    last = nc.tensor.transpose(turned_ps[:, q, a * P:(a + 1) * P],
                                               raw[:, p % RAW, a, q * P:(q + 1) * P], ident[:])
                if q % 2 == 1:
                    last.then_inc(turned, 1)

            def multiply_weights(t, p, tiles):
                c = ORDER[p % G]
                for q in tiles:
                    if q == 0:
                        pe.wait_ge(wt_done, t.blocks(p + 1))
                        if p == 0 and t.first >= 1:
                            pe.wait_ge(x1t_copied, t.row)
                    mm = nc.tensor.matmul(acc0[:], msg[:, c * T + q, :], wt[:, p % WTS, q, :],
                                          start=(p % G == 0 and q == 0), stop=(p % G == G - 1 and q == T - 1))
                    if q == T - 1:
                        mm.then_inc(acc0_done, 1)

            def mix_once(t, p):
                c, known = ORDER[p], at_once(t.known)
                begins, ends = sum(known[:p]) == 0, sum(known[p + 1:]) == 0
                pe.wait_ge(copied, t.blocks(p + 1, 2))
                if begins:
                    pe.wait_ge(added, t.tally(lambda k: per_step(ADDS, k)) + 1)
                if c == t.known - 1:
                    pe.wait_ge(sup_done, t.known)
                for q in range(T):
                    mm = nc.tensor.matmul(acc_once[:], support[:, c * T + q, :], kept[:, p % KEPT, q, :],
                                          start=(begins and q == 0), stop=(ends and q == T - 1))
                mm.then_inc(once_done, 1)

            def mix_late(t, j):
                _, r, c, begins, ends, bank = LATE[t.known][j]
                slot = j % LATE_SLOTS
                before = sum(n * len(LATE[k]) for f, n, k in PHASES if f < t.first) // LATE_SLOTS
                turn_loads = len(LATE[t.known]) // LATE_SLOTS
                pe.wait_ge(late_loaded[slot], (before + j // LATE_SLOTS + 1) * 16 + t.w * (16 * turn_loads))
                if c == t.known - 1:
                    pe.wait_ge(sup_done, t.known)
                if bank == 1:
                    pe.wait_ge(sup_done, t.row)
                if begins:
                    own = [i for i, a in enumerate(ADDS[t.known]) if a[2] == bank]
                    sums = [i for i, job in enumerate(LATE[t.known]) if job[3] and job[5] == bank]
                    k = sums.index(j)
                    pe.wait_ge(added, t.tally(lambda k: per_step(ADDS, k)) + 1 + (own[k - 1] + 1 if k else 0))
                acc = (acc_late, side)[bank]
                for q in range(T):
                    mm = nc.tensor.matmul(acc[:], support[:, c * T + q, :], late[:, slot, q, :],
                                          start=(begins and q == 0), stop=(ends and q == T - 1))
                mm.then_inc(late_done, 1)

            def turn_x1(g):
                pe.wait_ge(x1t_copied, g + 1)
                for a in range(T):
                    last = nc.tensor.transpose(side[:, a * P:(a + 1) * P], x1t[:, a * P:(a + 1) * P], ident[:])
                last.then_inc(x1_turned, 1)

            def turn_hid(g):
                pe.wait_ge(hid_done, g + 1)
                for a in range(T):
                    last = nc.tensor.transpose(side[:, a * P:(a + 1) * P], hid[:, a, :], ident[:])
                last.then_inc(hid_turned, 1)

            def multiply_support(g):
                pe.wait_ge(hid_t_done, g + 1)
                for a in range(T):
                    mm = nc.tensor.matmul(side[:, a * P:(a + 1) * P], hid_t[:, a * P:(a + 1) * P], w1t[:],
                                          start=True, stop=True)
                mm.then_inc(sup_multiplied, 1)

            def turn(t):
                for p in range(G):
                    n = t.first * G + p
                    for q in range(T):
                        turn_tile(t, p, q)
                    if t.first == 0:
                        turn_h0(p)
                        if n >= MUL_LAG:
                            multiply_weights(t, p - MUL_LAG, range(T))
                        multiply_msg(p)
                    if t.first >= 1 and p == 4:
                        turn_hid(t.row - 1)
                    if p >= 1 and at_once(t.known)[p - 1]:
                        mix_once(t, p - 1)
                    jobs = [j for j, job in enumerate(LATE[t.known]) if job[0] == p]
                    if jobs:
                        mix_late(t, jobs[0])
                    if t.first >= 1 and p == 3:
                        turn_x1(t.row - 1)
                    if t.first >= 1:
                        multiply_weights(t, p - MUL_LAG, range(T))
                    if t.first >= 1 and p == 4:
                        multiply_support(t.row - 1)
                    if jobs[1:]:
                        mix_late(t, jobs[1])

            pe.wait_ge(ident_done, 1)
            pe.wait_ge(x1_kept, 1)
            pe.wait_ge(w_loaded, 48)
            nc.tensor.matmul(acc_once[:, 0:D], ones_row[:], b_row[:], start=True, stop=True)
            nc.tensor.transpose(acc_late[:, 0:D], w1_sb[:], ident[:]).then_inc(small_mm, 1)
            pe.wait_ge(small_copied, 1)

            def turn_h0(p):
                c = ORDER[p]
                pe.wait_ge(h0_done, p + 1)
                for a in range(T):
                    last = nc.tensor.transpose(acc_once[:, a * P:(a + 1) * P], support[:, c * T + a, :], ident[:])
                last.then_inc(h0_turned, 1)

            def multiply_msg(p):
                pe.wait_ge(h0_t_done, p + 1)
                if p >= 1:
                    pe.wait_ge(msg_done, p)
                for a in range(T):
                    last = nc.tensor.matmul(acc_late[:, a * P:(a + 1) * P], hid_t[:, a * P:(a + 1) * P], w0_sb[:],
                                            start=True, stop=True)
                last.then_inc(m_multiplied, 1)

            turns(pe, turn, PHASES)

            def mix_end_block(j):
                r, c = END[j]
                i = NUM_LATE + j
                pe.wait_ge(late_loaded[i % LATE_SLOTS], (i // LATE_SLOTS + 1) * 16)
                if j == 0:
                    pe.wait_ge(copied, 2 * NB)
                if r >= T and c == LAST_KNOWN:
                    pe.wait_ge(end_added, r - T + 1)
                for q in range(T):
                    mm = nc.tensor.matmul(turned_ps[:, r % T, :], support[:, c * T + q, :],
                                          late[:, i % LATE_SLOTS, q, :],
                                          start=(c == LAST_KNOWN and q == 0), stop=(c == G - 1 and q == T - 1))
                mm.then_inc(late_done, 1)

            def turn_out(r):
                pe.wait_ge(end_added, r + 1)
                if r >= 2:
                    pe.wait_ge(out_summed, r - 1)
                bank = (acc_once, acc_late)[r % 2]
                for a in range(T):
                    last = nc.tensor.transpose(bank[:, a * P:(a + 1) * P], mix_end[:, r % 2, a * P:(a + 1) * P],
                                               ident[:])
                last.then_inc(mix_turned, 1)

            end = Turn(G, 0, G)
            for p in range(MUL_LAG):
                multiply_weights(end, p - MUL_LAG, range(T))
            outs = 0
            for j, (r, c) in enumerate(END):
                if j == T:
                    pe.wait_ge(sup_done, G)
                mix_end_block(j)
                if j == 0:
                    turn_x1(G - 1)
                if j == 1:
                    turn_hid(G - 1)
                if j == 2:
                    multiply_support(G - 1)
                if j >= T + 1 and outs < G and END[j - 1][1] == G - 1:
                    turn_out(END[j - 1][0])
                    outs += 1
            turn_out(G - 1)

        @block.scalar
        def _(act):
            def copy_half(t, p, half):
                n = t.first * G + p
                act.wait_ge(turned, t.blocks(p, 2) + half + 1)
                if half == 0 and n >= KEPT:
                    act.wait_ge(cut_done, t.blocks(p - KEPT + 1))
                    done = max(p - KEPT + 1, 0)
                    if t.known:
                        act.wait_ge(once_done, t.tally(at_once, done) + 1)
                    slot = p % KEPT
                    act.wait_ge(spilled[slot], t.tally(lambda k: stored(k, slot), done) * 16)
                q = half * 2
                nc.scalar.copy(kept[:, p % KEPT, q:q + 2, :], turned_ps[:, q:q + 2, :]).then_inc(copied, 1)

            def log(t, p):
                v = wt[:, p % WTS]
                act.wait_ge(cut_done, t.blocks(p + 1))
                nc.scalar.activation(v, v, ACT.Ln, bias=LN_GUARD).then_inc(ln_done, 1)

            def invert(t, p):
                v = wt[:, p % WTS]
                act.wait_ge(ln_done, t.blocks(p + 1))
                nc.scalar.activation(v, v, ACT.Exp, scale=-1.0).then_inc(inv_done, 1)

            def weigh(t, p):
                v = wt[:, p % WTS]
                act.wait_ge(quad_done, t.blocks(p + 1))
                nc.scalar.activation(v, v, ACT.Exp, scale=-2.0, bias=-2.0).then_inc(wt_done, 1)

            def end_rows(g):
                act.wait_ge(hid_turned, g + 1)
                nc.scalar.copy(hid_t[:], side[:]).then_inc(hid_t_done, 1)
                act.wait_ge(pows_done, g + 1)
                nc.scalar.activation(inv[:], pows[:], ACT.Ln).then_inc(pows_ln, 1)
                act.wait_ge(pows_ln, g + 1)
                nc.scalar.activation(inv[:], inv[:], ACT.Exp, scale=-0.5).then_inc(pows_exp, 1)

            def turn(t):
                for p in range(G):
                    n = t.first * G + p
                    copy_half(t, p, 0)
                    if t.first == 0:
                        act.wait_ge(h0_turned, p + 1)
                        if p >= 1:
                            act.wait_ge(m_multiplied, p)
                        nc.scalar.copy(hid_t[:], acc_once[:]).then_inc(h0_t_done, 1)
                    copy_half(t, p, 1)
                    if n >= 2:
                        weigh(t, p - 2)
                    if t.first >= 1 and p == 4:
                        end_rows(t.row - 1)
                    if n >= 1:
                        log(t, p - 1)
                        invert(t, p - 1)

            nc.scalar.preload_act_table_set("natural_log_exp_and_others")
            act.wait_ge(small_mm, 1)
            nc.scalar.copy(w1t[:], acc_late[:, 0:D])
            nc.scalar.copy(b_all[:], acc_once[:, 0:D]).then_inc(small_copied, 1)
            act.wait_ge(var_all, 1)
            nc.scalar.activation(rs0[:], var0[:], ACT.Ln).then_inc(ln_all, 1)
            act.wait_ge(ln_all, 1)
            nc.scalar.activation(rs0[:], rs0[:], ACT.Exp, scale=-0.5).then_inc(exp_all, 1)
            turns(act, turn, PHASES)
            end = Turn(G, 0, G)
            weigh(end, -2)
            log(end, -1)
            invert(end, -1)
            weigh(end, -1)
            end_rows(G - 1)

        @block.vector
        def _(dve):
            def row_sum(t, p):
                n = t.first * G + p
                dve.wait_ge(raw_loaded[p % RAW], (n // RAW + 1) * 16 + t.w * (16 * G // RAW))
                if p == 0 and t.first >= 1:
                    dve.wait_ge(rows_summed, t.row)
                nc.vector.tensor_reduce(rowpart[:, :, p:p + 1], raw[:, p % RAW], AX_X, ALU.add).then_inc(summed, 1)
                if p == G - 1:
                    dve.wait_ge(summed, t.blocks(p + 1))
                    if t.first >= 1:
                        dve.wait_ge(pows_ln, t.row)
                    nc.vector.tensor_reduce(pows[:, 0, :], rowpart[:], AX_X, ALU.add).then_inc(rows_summed, 1)

            def cut(t, p):
                v = kept[:, p % KEPT]
                dve.wait_ge(copied, t.blocks(p + 1, 2))
                if t.first * G + p >= WTS:
                    dve.wait_ge(acc0_done, t.blocks(p - WTS + 1))
                nc.vector.scalar_tensor_tensor(out=wt[:, p % WTS], in0=v, scalar=CUTOFF, in1=v, op0=ALU.is_lt,
                                               op1=ALU.mult).then_inc(cut_done, 1)

            def quad(t, p):
                v = wt[:, p % WTS]
                dve.wait_ge(inv_done, t.blocks(p + 1))
                nc.vector.scalar_tensor_tensor(out=v, in0=v, scalar=-2.0, in1=v, op0=ALU.add,
                                               op1=ALU.mult).then_inc(quad_done, 1)

            def add_sum(t, i):
                _, r, bank = ADDS[t.known][i]
                if r == "once":
                    dve.wait_ge(once_done, t.tally(at_once, G) + 1)
                    acc, row = acc_once, t.row
                else:
                    nth = sum(a[1] != "once" for a in ADDS[t.known][:i])
                    j = [j for j, job in enumerate(LATE[t.known]) if job[4]][nth]
                    dve.wait_ge(late_done, t.tally(lambda k: per_step(LATE, k)) + j + 2)
                    acc, row = (acc_late, side)[bank], t.w * SHARE[t.known] + r
                dve.wait_ge(added, t.tally(lambda k: per_step(ADDS, k)) + i + 1)
                rows = mixed[:, bass.ds(row, 1), :] if not isinstance(row, int) else mixed[:, row:row + 1, :]
                nc.vector.tensor_tensor(rows, acc[:].rearrange("d (a i) -> d a i", a=1), rows,
                                        ALU.add).then_inc(added, 1)

            def copy_x1t(g):
                dve.wait_ge(acc0_done, (g + 1) * G)
                nc.vector.tensor_copy(x1t[:], acc0[:]).then_inc(x1t_copied, 1)

            def end_rows(g):
                dve.wait_ge(x1_turned, g + 1)
                dve.wait_ge(x1_kept, g + 1)
                rows = x1[:, bass.ds(g * T, T), :]
                nc.vector.tensor_tensor(x1_now[:], side[:].rearrange("p (a d) -> p a d", a=T), rows,
                                        ALU.add).then_inc(x1_done, 1)
                dve.wait_ge(x1_done, g + 1)
                for a in range(T):
                    last = nc.vector.bn_stats(bn[:, a, :], x1_now[:, a, :])
                last.then_inc(stats_done, 1)
                dve.wait_ge(rows_summed, g + 1)
                dve.wait_ge(stats_done, g + 1)
                nc.vector.tensor_scalar(pows[:, 0, :], pows[:, 0, :], 1.0, None, ALU.add)
                for a in range(T):
                    last = nc.vector.bn_aggr(mv[:, a, :], bn[:, a, :])
                last.then_inc(moments_done, 1)
                dve.wait_ge(moments_done, g + 1)
                for a in range(T):
                    last = nc.vector.tensor_scalar(hid[:, a, :], x1_now[:, a, :], mv[:, a, 0:1], 0.0,
                                                   ALU.subtract, ALU.max)
                last.then_inc(hid_done, 1)
                nc.vector.tensor_scalar(pows[:, 1, :], mv[:, 0:T, 1], EPS, None, ALU.add).then_inc(pows_done, 1)

            def newton_step(y, a, tmp, done, before):
                nc.vector.tensor_tensor(tmp, y, y, ALU.mult).then_inc(done, 1)
                dve.wait_ge(done, before + 1)
                nc.vector.scalar_tensor_tensor(out=tmp, in0=tmp, scalar=-0.5, in1=a, op0=ALU.mult,
                                               op1=ALU.mult).then_inc(done, 1)
                dve.wait_ge(done, before + 2)
                nc.vector.scalar_tensor_tensor(out=y, in0=tmp, scalar=1.5, in1=y, op0=ALU.add,
                                               op1=ALU.mult).then_inc(done, 1)
                dve.wait_ge(done, before + 3)

            def make_support(g):
                dve.wait_ge(pows_exp, g + 1)
                newton_step(inv[:], pows[:], tmp1[:], newton, g * 3)
                nc.vector.tensor_copy(dinv[:, bass.ds(g * T, T)], inv[:, 0, :]).then_inc(dinv_done, 1)
                nc.vector.tensor_tensor(scale[:], inv[:, 0, :], inv[:, 1, :], ALU.mult).then_inc(scale_done, 1)
                dve.wait_ge(scale_done, g + 1)
                dve.wait_ge(sup_multiplied, g + 1)
                for a in range(T):
                    last = nc.vector.tensor_scalar(support[:, bass.ds(g * T + a, 1), :], side[:, a * P:(a + 1) * P],
                                                   scale[:, a:a + 1], None, ALU.mult)
                last.then_inc(sup_done, 1)

            def make_h0(p):
                for a in range(ORDER[p] * T, ORDER[p] * T + T):
                    last = nc.vector.tensor_scalar(support[:, a, :], x1[:, a, :], mv[:, a, 0:1], 0.0,
                                                   ALU.subtract, ALU.max)
                last.then_inc(h0_done, 1)

            def make_msg(p):
                dve.wait_ge(m_multiplied, p + 1)
                for a in range(T):
                    n = ORDER[p] * T + a
                    last = nc.vector.scalar_tensor_tensor(out=msg[:, n, :], in0=acc_late[:, a * P:(a + 1) * P],
                                                          scalar=rs0[:, n:n + 1], in1=b_all[:], op0=ALU.mult,
                                                          op1=ALU.add)
                last.then_inc(msg_done, 1)

            def turn(t):
                for p in range(G):
                    n = t.first * G + p
                    if t.first >= 1 and p == 3:
                        copy_x1t(t.row - 1)
                    if n >= 2:
                        quad(t, p - 2)
                    for i, a in enumerate(ADDS[t.known]):
                        if a[0] == p:
                            add_sum(t, i)
                    if t.first >= 1 and p == 3:
                        end_rows(t.row - 1)
                    if t.first == 0 and p + 1 < G:
                        make_h0(p + 1)
                    row_sum(t, p)
                    cut(t, p)
                    if t.first >= 1 and p == 4:
                        make_support(t.row - 1)
                    if t.first == 0:
                        make_msg(p)
                for i, a in enumerate(ADDS[t.known]):
                    if a[0] == G:
                        add_sum(t, i)

            for h in range(2):
                dve.wait_ge(x_loaded, 32)
                for a in range(h * NT // 2, (h + 1) * NT // 2):
                    last = nc.vector.bn_stats(bn[:, a, :], x1[:, a, :])
            last.then_inc(bn_all, 1)
            dve.wait_ge(bn_all, 1)
            for a in range(NT):
                last = nc.vector.bn_aggr(mv[:, a, :], bn[:, a, :])
            last.then_inc(mv_all, 1)
            dve.wait_ge(mv_all, 1)
            nc.vector.tensor_scalar(var0[:], mv[:, :, 1], EPS, None, ALU.add).then_inc(var_all, 1)
            make_h0(0)
            dve.wait_ge(exp_all, 1)
            newton_step(rs0[:], var0[:], tmp0[:], newton_all, 0)
            dve.wait_ge(small_copied, 1)
            turns(dve, turn, PHASES)

            end = Turn(G, 0, G)
            quad(end, -2)
            quad(end, -1)
            copy_x1t(G - 1)
            end_rows(G - 1)
            make_support(G - 1)

            def add_end(r):
                dve.wait_ge(late_done, NUM_LATE + 2 + END.index((r, G - 1)))
                dve.wait_ge(added, NUM_ADDS + 1)
                if r >= 2:
                    dve.wait_ge(mix_turned, r - 1)
                nc.vector.tensor_tensor(mix_end[:, r % 2, :], turned_ps[:, r % T, :], mixed[:, r, :],
                                        ALU.add).then_inc(end_added, 1)

            def finish(r):
                dve.wait_ge(mix_turned, r + 1)
                if r == 0:
                    dve.wait_ge(x1_kept, G + 1)
                    dve.wait_ge(sup_done, G)
                    dve.wait_ge(dinv_done, G)
                if r >= 2:
                    dve.wait_ge(out_written[r % 2], 16 * (r // 2))
                rows = slice(r * T, r * T + T)
                bank = (acc_once, acc_late)[r % 2]
                nc.vector.tensor_tensor(fin[:, r % 2], bank[:].rearrange("p (a d) -> p a d", a=T),
                                        support[:, rows, :], ALU.add).then_inc(out_summed, 1)
                dve.wait_ge(out_summed, r + 1)
                for a in range(T):
                    last = nc.vector.tensor_scalar(fin[:, r % 2, a, :], fin[:, r % 2, a, :],
                                                   dinv[:, r * T + a:r * T + a + 1], 0.0, ALU.mult, ALU.max)
                last.then_inc(out_relu, 1)
                dve.wait_ge(out_relu, r + 1)
                nc.vector.tensor_tensor(fin[:, r % 2], fin[:, r % 2], x1[:, rows, :], ALU.add).then_inc(out_done, 1)

            for r in range(G):
                add_end(r)
                if r >= 1:
                    finish(r - 1)
            finish(G - 1)


_INS = ["x", "adj", "L0_gnn_W", "L0_gnn_B", "L1_gnn_W"]


def kernel(**inputs):
    import numpy as _np
    import concourse.bacc as _bacc
    from concourse import mybir as _mybir
    from concourse.bass_utils import run_bass_kernel_spmd as _run

    nc = _bacc.Bacc("TRN2", target_bir_lowering=False, num_devices=1)
    arrays, args = {}, []
    for name in _INS:
        a = _np.ascontiguousarray(inputs[name])
        arrays[f"in_{name}_dram"] = a
        args.append(nc.dram_tensor(f"in_{name}_dram", a.shape, _mybir.dt.from_np(a.dtype), kind="ExternalInput").ap())
    shape = inputs["x"].shape
    args.append(nc.dram_tensor("out_0_dram", shape, _mybir.dt.float32, kind="ExternalOutput").ap())
    build(nc, *args)
    r = _run(nc, [arrays], core_ids=[0])
    return r.results[0]["out_0_dram"]
```

```python
from contextlib import ExitStack

import concourse.bass as bass
from concourse import mybir

P = 128
F32 = mybir.dt.float32
ALU = mybir.AluOpType
ACT = mybir.ActivationFunctionType
AX_X = mybir.AxisListType.X

EPS = 1e-5
CUTOFF = 1.0
LN_GUARD = 2.0 ** -30

G = 8
ORDER = [1, 3, 4, 0, 7, 2, 5, 6]
MIX_STEP = [1, 2, 3, 5, 5, 6, 7, None]
PHASES = [(0, 1, 0), (1, 2, 1), (3, 3, 3), (6, 2, 6)]
LATE = {
    0: [],
    1: [],
    3: [(3, 0, 1, True, False, 0), (7, 0, 2, False, True, 0)],
    6: [(0, 0, 3, True, False, 0), (1, 0, 4, False, True, 0), (2, 1, 3, True, False, 0), (3, 1, 4, False, True, 0),
        (4, 2, 3, True, False, 0), (4, 2, 4, False, True, 0), (5, 0, 5, True, True, 1), (6, 1, 5, True, True, 0),
        (7, 2, 5, True, True, 1)],
}
SHARE = {3: 1, 6: 3}
END_FIRST = (0, 0)
ADDS = {
    0: [],
    1: [(6, "once", None)],
    3: [(7, "once", None), (G, 0, 0)],
    6: [(2, 0, 0), (4, 1, 0), (5, 2, 0), (6, 0, 1), (7, 1, 0), (G, "once", None), (G, 2, 1)],
}
LATE_SLOTS = 3
RAW, KEPT, WTS = 4, 4, 4
AHEAD = 3
X_PARTS = 4
MESSAGES = [[], [], [0], [1, 2], [3], [4], [5, 6], [7]]
MUL_LAG = 3


def stored(known, slot=None):
    return [int(c >= known and slot in (None, p % KEPT)) for p, c in enumerate(ORDER)]


def at_once(known):
    return [int(c < known) for c in ORDER]


def per_step(items, known):
    return [sum(min(i[0], G - 1) == p for i in items[known]) for p in range(G)]


def late_slot(known, j):
    return (j - len(LATE[known])) % LATE_SLOTS


def slot_loads(known, slot):
    return [sum(min(job[0], G - 1) == p and late_slot(known, j) == slot for j, job in enumerate(LATE[known]))
            for p in range(G)]


class Turn:

    def __init__(self, first, w, known):
        self.first, self.w, self.known = first, w, known
        self.row = first + w

    def blocks(self, p, per=1):
        return (self.first * G + p) * per + self.w * (G * per)

    def tally(self, events, p=0):
        before = sum(sum(events(k)) * n for f, n, k in PHASES if f < self.first)
        return before + self.w * sum(events(self.known)) + sum(events(self.known)[:p])


def build(nc, x, adj, w0, b0, w1, out):
    N, D = x.shape
    ROWS = N // G
    T = ROWS // P
    NT = N // P
    NB = G * G

    ctx = ExitStack()
    with ctx:
        def sb(name, shape):
            return ctx.enter_context(nc.sbuf_tensor(name, shape, F32))

        def ps(name, shape):
            return ctx.enter_context(nc.psum_tensor(name, shape, F32))

        def sem(name):
            return ctx.enter_context(nc.semaphore(name))

        spill = nc.dram_tensor("adj_t_spill", [G, G + 1, P, T, ROWS], F32, kind="Internal").ap()

        ident = sb("ident", [P, P])
        ones_row = sb("ones_row", [1, P])
        w0_sb = sb("w0_sb", [D, D])
        w1_sb = sb("w1_sb", [D, D])
        w1t = sb("w1t", [D, D])
        b_row = sb("b_row", [1, D])
        b_all = sb("b_all", [P, D])
        x1 = sb("x1", [P, NT, D])
        msg = sb("msg", [P, NT, D])
        support = sb("support", [P, NT, D])
        mixed = sb("mixed", [D, G, ROWS])
        raw = sb("raw", [P, RAW, T, ROWS])
        kept = sb("kept", [P, KEPT, T, ROWS])
        late = sb("late", [P, LATE_SLOTS, T, ROWS])
        wt = sb("wt", [P, WTS, T, ROWS])
        x1t = sb("x1t", [D, ROWS])
        x1_now = sb("x1_now", [P, T, D])
        hid = sb("hid", [P, T, D])
        hid_t = sb("hid_t", [D, ROWS])
        bn = sb("bn", [P, NT, 6])
        mv = sb("mv", [P, NT, 2])
        var0 = sb("var0", [P, NT])
        rs0 = sb("rs0", [P, NT])
        tmp0 = sb("tmp0", [P, NT])
        rowpart = sb("rowpart", [P, T, G])
        pows = sb("pows", [P, 2, T])
        inv = sb("inv", [P, 2, T])
        tmp1 = sb("tmp1", [P, 2, T])
        scale = sb("scale", [P, T])
        dinv = sb("dinv", [P, NT])
        mix_end = sb("mix_end", [D, 2, ROWS])
        fin = sb("fin", [P, 2, T, D])

        turned_ps = ps("turned_ps", [P, T, ROWS])
        acc0 = ps("acc0", [D, ROWS])
        acc_once = ps("acc_once", [D, ROWS])
        acc_late = ps("acc_late", [D, ROWS])
        side = ps("side", [P, ROWS])

        msg_banks = (acc_once, side)
        h0_t = (hid_t, x1t)

        x_loaded = [sem(f"x_loaded{i}") for i in range(X_PARTS)]
        w_loaded = sem("w_loaded")
        raw_loaded = [sem(f"raw_loaded{i}") for i in range(RAW)]
        spilled = [sem(f"spilled{i}") for i in range(KEPT)]
        late_loaded = [sem(f"late_loaded{i}") for i in range(LATE_SLOTS)]
        out_written = [sem(f"out_written{i}") for i in range(2)]
        ident_zeroed = sem("ident_zeroed")
        ident_done = sem("ident_done")
        turned = sem("turned")
        copied = sem("copied")
        summed = sem("summed")
        cut_done = sem("cut_done")
        ln_done = sem("ln_done")
        inv_done = sem("inv_done")
        quad_done = sem("quad_done")
        wt_done = sem("wt_done")
        acc0_done = sem("acc0_done")
        once_done = sem("once_done")
        late_done = sem("late_done")
        added = sem("added")
        x1_kept = sem("x1_kept")
        rows_summed = sem("rows_summed")
        x1t_copied = sem("x1t_copied")
        x1_turned = sem("x1_turned")
        x1_done = sem("x1_done")
        stats_done = sem("stats_done")
        moments_done = sem("moments_done")
        pows_done = sem("pows_done")
        pows_ln = sem("pows_ln")
        pows_exp = sem("pows_exp")
        newton = sem("newton")
        dinv_done = sem("dinv_done")
        scale_done = sem("scale_done")
        hid_done = sem("hid_done")
        hid_turned = sem("hid_turned")
        hid_t_done = sem("hid_t_done")
        sup_multiplied = sem("sup_multiplied")
        sup_done = sem("sup_done")
        small_mm = sem("small_mm")
        small_copied = sem("small_copied")
        bn_all = sem("bn_all")
        mv_all = sem("mv_all")
        var_all = sem("var_all")
        ln_all = sem("ln_all")
        exp_all = sem("exp_all")
        newton_all = sem("newton_all")
        h0_done = sem("h0_done")
        h0_turned = sem("h0_turned")
        h0_t_done = sem("h0_t_done")
        m_multiplied = sem("m_multiplied")
        msg_done = sem("msg_done")
        end_added = sem("end_added")
        mix_turned = sem("mix_turned")
        out_summed = sem("out_summed")
        out_relu = sem("out_relu")
        out_done = sem("out_done")

        adj_blocks = adj.rearrange("(g a p) (c j) -> g c p a j", a=T, p=P, j=ROWS)
        x_rows = x.rearrange("(t p) d -> p t d", p=P)
        out_rows = out.rearrange("(g a p) d -> g p a d", a=T, p=P)

        NUM_ADDS = sum(n * len(ADDS[k]) for _, n, k in PHASES)
        NUM_LATE = sum(n * len(LATE[k]) for _, n, k in PHASES)
        LAST_KNOWN = PHASES[-1][2]
        END = [END_FIRST] + [(r, c) for rows in (range(T), range(T, G)) for c in range(LAST_KNOWN, G) for r in rows]

        def turns(eng, turn, phases):
            for first, n, known in phases:
                if n == 1:
                    turn(Turn(first, 0, known))
                else:
                    with eng.Fori(0, n) as w:
                        turn(Turn(first, w, known))

        block = ctx.enter_context(nc.Block())

        @block.sync
        def _(sp):
            def load(t, p, n):
                if n >= RAW:
                    sp.wait_ge(cut_done, t.blocks(p - RAW + 1))
                sp.dma_start(raw[:, p % RAW], adj_blocks[t.row + p // G, ORDER[p % G]]).then_inc(raw_loaded[p % RAW], 16)

            def store(t, p):
                sp.wait_ge(copied, t.blocks(p + 1, 2))
                sp.dma_start(spill[t.row, 1 + ORDER[p]], kept[:, p % KEPT]).then_inc(spilled[p % KEPT], 16)

            def turn(t, last=False):
                for p in range(G):
                    if not (last and p + AHEAD >= G):
                        load(t, p + AHEAD, t.first * G + p + AHEAD)
                    if stored(t.known)[p]:
                        store(t, p)

            sp.dma_start(w0_sb[:], w0).then_inc(w_loaded, 16)
            sp.dma_start(w1_sb[:], w1).then_inc(w_loaded, 16)
            sp.dma_start(b_row[:], b0.rearrange("(a d) -> a d", a=1)).then_inc(w_loaded, 16)
            first = Turn(0, 0, 0)
            load(first, 0, 0)
            for i in range(X_PARTS):
                part = slice(i * NT // X_PARTS, (i + 1) * NT // X_PARTS)
                sp.dma_start(x1[:, part], x_rows[:, part]).then_inc(x_loaded[i], 16)
            for n in range(1, AHEAD):
                load(first, n, n)
            turns(sp, turn, PHASES[:-1])
            f, n, known = PHASES[-1]
            turn(Turn(f, 0, known))
            turn(Turn(f, 1, known), last=True)
            for r in range(G):
                sp.wait_ge(out_done, r + 1)
                sp.dma_start(out_rows[r], fin[:, r % 2]).then_inc(out_written[r % 2], 16)
            for b in range(2):
                sp.wait_ge(out_written[b], 16 * (G // 2))

        @block.gpsimd
        def _(pool):
            nc.gpsimd.memset(ident[:], 0.0).then_inc(ident_zeroed, 1)
            nc.gpsimd.memset(ones_row[:], 1.0).then_inc(x1_kept, 1)
            pool.wait_ge(ident_zeroed, 1)
            nc.gpsimd.affine_select(out=ident[:], in_=ident[:], compare_op=ALU.not_equal, fill=1.0, base=0,
                                    pattern=[[-1, P]], channel_multiplier=1).then_inc(ident_done, 1)
            nc.gpsimd.memset(mixed[:, 0:G // 2], 0.0).then_inc(once_done, 1)
            nc.gpsimd.memset(mixed[:, G // 2:G - 1], 0.0).then_inc(late_done, LATE_SLOTS)
            nc.gpsimd.memset(mixed[:, G - 1:G], 0.0).then_inc(added, 1)

            pool.wait_ge(h0_done, 1)
            for p in range(1, G):
                for a in range(ORDER[p] * T, ORDER[p] * T + T):
                    last = nc.gpsimd.tensor_scalar(support[:, a, :], x1[:, a, :], mv[:, a, 0:1], 0.0,
                                                   ALU.subtract, ALU.max)
                last.then_inc(h0_done, 1)

            def keep_x1(g):
                pool.wait_ge(x1_done, g + 1)
                nc.gpsimd.tensor_copy(x1[:, bass.ds(g * T, T), :], x1_now[:]).then_inc(x1_kept, 1)

            def load_late(t, j):
                _, r, c, _, _, _ = LATE[t.known][j]
                slot = late_slot(t.known, j)
                pool.wait_ge(late_done, t.tally(lambda k: per_step(LATE, k)) + 1 + (j if j >= LATE_SLOTS else slot))
                pool.dma_start(late[:, slot], spill[t.w * SHARE[t.known] + r, 1 + c]).then_inc(late_loaded[slot], 16)

            def wait_spilled(first):
                for slot in range(KEPT):
                    pool.wait_ge(spilled[slot], 16 * sum(n * sum(stored(k, slot)) for f, n, k in PHASES if f < first))

            def turn(t):
                for j, job in enumerate(LATE[t.known]):
                    if job[0] <= 5:
                        load_late(t, j)
                if t.first >= 1:
                    keep_x1(t.row - 1)
                for j, job in enumerate(LATE[t.known]):
                    if job[0] > 5:
                        load_late(t, j)
                if LATE[t.known]:
                    wait_spilled(t.first)

            for phase in PHASES:
                if LATE[phase[2]]:
                    wait_spilled(SHARE[phase[2]])
                turns(pool, turn, [phase])
            wait_spilled(G)
            for j, (r, c) in enumerate(END):
                if j == LATE_SLOTS:
                    keep_x1(G - 1)
                pool.wait_ge(late_done, NUM_LATE + j + 1)
                slot = j % LATE_SLOTS
                pool.dma_start(late[:, slot], spill[r, 1 + c]).then_inc(late_loaded[slot], 16)

        @block.tensor
        def _(pe):
            def turn_tile(t, p, q):
                n = t.first * G + p
                if q == 0:
                    pe.wait_ge(raw_loaded[p % RAW], (n // RAW + 1) * 16 + t.w * (16 * G // RAW))
                if q % 2 == 0 and n >= 1:
                    pe.wait_ge(copied, t.blocks(p - 1, 2) + q // 2 + 1)
                for a in range(T):
                    last = nc.tensor.transpose(turned_ps[:, q, a * P:(a + 1) * P],
                                               raw[:, p % RAW, a, q * P:(q + 1) * P], ident[:])
                if q % 2 == 1:
                    last.then_inc(turned, 1)

            def multiply_weights(t, p, tiles):
                c = ORDER[p % G]
                for q in tiles:
                    if q == 0:
                        pe.wait_ge(wt_done, t.blocks(p + 1))
                        if t.first == 0:
                            pe.wait_ge(msg_done, p + 1)
                        if p == 0 and t.first >= 1:
                            pe.wait_ge(x1t_copied, t.row)
                    mm = nc.tensor.matmul(acc0[:], msg[:, c * T + q, :], wt[:, p % WTS, q, :],
                                          start=(p % G == 0 and q == 0), stop=(p % G == G - 1 and q == T - 1))
                    if q == T - 1:
                        mm.then_inc(acc0_done, 1)

            def mix_once(t, p):
                c, known = ORDER[p], at_once(t.known)
                begins, ends = sum(known[:p]) == 0, sum(known[p + 1:]) == 0
                pe.wait_ge(copied, t.blocks(p + 1, 2))
                if begins:
                    pe.wait_ge(added, t.tally(lambda k: per_step(ADDS, k)) + 1)
                if c == t.known - 1:
                    pe.wait_ge(sup_done, t.known)
                for q in range(T):
                    mm = nc.tensor.matmul(acc_once[:], support[:, c * T + q, :], kept[:, p % KEPT, q, :],
                                          start=(begins and q == 0), stop=(ends and q == T - 1))
                mm.then_inc(once_done, 1)

            def mix_late(t, j):
                _, r, c, begins, ends, bank = LATE[t.known][j]
                slot = late_slot(t.known, j)
                nth = t.tally(lambda k: slot_loads(k, slot)) + j // LATE_SLOTS + 1
                pe.wait_ge(late_loaded[slot], nth * 16)
                if c == t.known - 1:
                    pe.wait_ge(sup_done, t.known)
                if bank == 1:
                    pe.wait_ge(sup_done, t.row)
                if begins:
                    own = [i for i, a in enumerate(ADDS[t.known]) if a[2] == bank]
                    sums = [i for i, job in enumerate(LATE[t.known]) if job[3] and job[5] == bank]
                    k = sums.index(j)
                    pe.wait_ge(added, t.tally(lambda k: per_step(ADDS, k)) + 1 + (own[k - 1] + 1 if k else 0))
                acc = (acc_late, side)[bank]
                for q in range(T):
                    mm = nc.tensor.matmul(acc[:], support[:, c * T + q, :], late[:, slot, q, :],
                                          start=(begins and q == 0), stop=(ends and q == T - 1))
                mm.then_inc(late_done, 1)

            def turn_x1(g):
                pe.wait_ge(x1t_copied, g + 1)
                for a in range(T):
                    last = nc.tensor.transpose(side[:, a * P:(a + 1) * P], x1t[:, a * P:(a + 1) * P], ident[:])
                last.then_inc(x1_turned, 1)

            def turn_hid(g):
                pe.wait_ge(hid_done, g + 1)
                for a in range(T):
                    last = nc.tensor.transpose(side[:, a * P:(a + 1) * P], hid[:, a, :], ident[:])
                last.then_inc(hid_turned, 1)

            def multiply_support(g):
                pe.wait_ge(hid_t_done, g + 1)
                for a in range(T):
                    mm = nc.tensor.matmul(side[:, a * P:(a + 1) * P], hid_t[:, a * P:(a + 1) * P], w1t[:],
                                          start=True, stop=True)
                mm.then_inc(sup_multiplied, 1)

            def turn(t):
                for p in range(G):
                    n = t.first * G + p
                    for q in range(T):
                        turn_tile(t, p, q)
                    if t.first == 0:
                        for m in MESSAGES[p]:
                            turn_h0(m)
                        if n >= MUL_LAG:
                            multiply_weights(t, p - MUL_LAG, range(T))
                        for m in MESSAGES[p]:
                            multiply_msg(m)
                    if t.first >= 1 and p == 5:
                        multiply_support(t.row - 1)
                    once = [b for b in range(G) if at_once(t.known)[b] and MIX_STEP[b] == p]
                    jobs = [j for j, job in enumerate(LATE[t.known]) if job[0] == p]
                    first = [] if p in (4, 5) else jobs[:1]
                    if once and p != 5:
                        mix_once(t, once[0])
                    for j in first:
                        mix_late(t, j)
                    if t.first >= 1 and p == 3:
                        turn_x1(t.row - 1)
                    if t.first >= 1:
                        multiply_weights(t, p - MUL_LAG, range(T))
                    if t.first >= 1 and p == 4:
                        turn_hid(t.row - 1)
                    if once and p == 5:
                        mix_once(t, once[0])
                    for j in jobs[len(first):]:
                        mix_late(t, j)

            pe.wait_ge(ident_done, 1)
            pe.wait_ge(x1_kept, 1)
            pe.wait_ge(w_loaded, 48)
            nc.tensor.matmul(acc_once[:, 0:D], ones_row[:], b_row[:], start=True, stop=True)
            nc.tensor.transpose(acc_late[:, 0:D], w1_sb[:], ident[:]).then_inc(small_mm, 1)
            pe.wait_ge(small_copied, 1)

            def turn_h0(m):
                c = ORDER[m]
                pe.wait_ge(h0_done, m + 1)
                if m >= 2:
                    pe.wait_ge(msg_done, m - 1)
                for a in range(T):
                    last = nc.tensor.transpose(msg_banks[m % 2][:, a * P:(a + 1) * P], support[:, c * T + a, :],
                                               ident[:])
                last.then_inc(h0_turned, 1)

            def multiply_msg(m):
                pe.wait_ge(h0_t_done, m + 1)
                for a in range(T):
                    last = nc.tensor.matmul(msg_banks[m % 2][:, a * P:(a + 1) * P],
                                            h0_t[m % 2][:, a * P:(a + 1) * P], w0_sb[:], start=True, stop=True)
                last.then_inc(m_multiplied, 1)

            turns(pe, turn, PHASES)

            def mix_end_block(j):
                r, c = END[j]
                slot = j % LATE_SLOTS
                before = sum(n * sum(slot_loads(k, slot)) for _, n, k in PHASES)
                pe.wait_ge(late_loaded[slot], (before + j // LATE_SLOTS + 1) * 16)
                if j == 0:
                    pe.wait_ge(copied, 2 * NB)
                if r >= T and (r, c) in begins:
                    pe.wait_ge(end_added, r - T + 1)
                for q in range(T):
                    mm = nc.tensor.matmul(turned_ps[:, r % T, :], support[:, c * T + q, :],
                                          late[:, slot, q, :],
                                          start=((r, c) in begins and q == 0), stop=(c == G - 1 and q == T - 1))
                mm.then_inc(late_done, 1)

            def turn_out(r):
                pe.wait_ge(end_added, r + 1)
                if r >= 2:
                    pe.wait_ge(out_summed, r - 1)
                bank = (acc_once, acc_late)[r % 2]
                for a in range(T):
                    last = nc.tensor.transpose(bank[:, a * P:(a + 1) * P], mix_end[:, r % 2, a * P:(a + 1) * P],
                                               ident[:])
                last.then_inc(mix_turned, 1)

            begins = [END_FIRST] + [(r, LAST_KNOWN) for r in range(G) if r != END_FIRST[0]]
            end = Turn(G, 0, G)
            for p in range(MUL_LAG):
                multiply_weights(end, p - MUL_LAG, range(T))
            outs = 0
            for j, (r, c) in enumerate(END):
                if j == T + 1:
                    pe.wait_ge(sup_done, G)
                mix_end_block(j)
                if j == 0:
                    turn_x1(G - 1)
                if j == 1:
                    turn_hid(G - 1)
                if j == 2:
                    multiply_support(G - 1)
                if j >= T + 2 and outs < G and END[j - 1][1] == G - 1:
                    turn_out(END[j - 1][0])
                    outs += 1
            turn_out(G - 1)

        @block.scalar
        def _(act):
            def copy_half(t, p, half):
                n = t.first * G + p
                act.wait_ge(turned, t.blocks(p, 2) + half + 1)
                if half == 0 and n >= KEPT:
                    act.wait_ge(cut_done, t.blocks(p - KEPT + 1))
                    done = max(p - KEPT + 1, 0)
                    if t.known:
                        act.wait_ge(once_done, t.tally(at_once, done) + 1)
                    slot = p % KEPT
                    act.wait_ge(spilled[slot], t.tally(lambda k: stored(k, slot), done) * 16)
                q = half * 2
                nc.scalar.copy(kept[:, p % KEPT, q:q + 2, :], turned_ps[:, q:q + 2, :]).then_inc(copied, 1)

            def log(t, p):
                v = wt[:, p % WTS]
                act.wait_ge(cut_done, t.blocks(p + 1))
                nc.scalar.activation(v, v, ACT.Ln, bias=LN_GUARD).then_inc(ln_done, 1)

            def invert(t, p):
                v = wt[:, p % WTS]
                act.wait_ge(ln_done, t.blocks(p + 1))
                nc.scalar.activation(v, v, ACT.Exp, scale=-1.0).then_inc(inv_done, 1)

            def weigh(t, p):
                v = wt[:, p % WTS]
                act.wait_ge(quad_done, t.blocks(p + 1))
                nc.scalar.activation(v, v, ACT.Exp, scale=-2.0, bias=-2.0).then_inc(wt_done, 1)

            def copy_hid(g):
                act.wait_ge(hid_turned, g + 1)
                nc.scalar.copy(hid_t[:], side[:]).then_inc(hid_t_done, 1)

            def log_pows(g):
                act.wait_ge(pows_done, g + 1)
                nc.scalar.activation(inv[:], pows[:], ACT.Ln).then_inc(pows_ln, 1)

            def exp_pows(g):
                act.wait_ge(pows_ln, g + 1)
                nc.scalar.activation(inv[:], inv[:], ACT.Exp, scale=-0.5).then_inc(pows_exp, 1)

            def std_rows():
                act.wait_ge(var_all, 1)
                nc.scalar.activation(rs0[:], var0[:], ACT.Ln).then_inc(ln_all, 1)
                act.wait_ge(ln_all, 1)
                nc.scalar.activation(rs0[:], rs0[:], ACT.Exp, scale=-0.5).then_inc(exp_all, 1)

            def copy_h0(m):
                act.wait_ge(h0_turned, m + 1)
                if m >= 2:
                    act.wait_ge(m_multiplied, m - 1)
                nc.scalar.copy(h0_t[m % 2][:], msg_banks[m % 2][:]).then_inc(h0_t_done, 1)

            def turn(t):
                for p in range(G):
                    n = t.first * G + p
                    copy_half(t, p, 0)
                    copy_half(t, p, 1)
                    if n >= 1:
                        log(t, p - 1)
                    if n == 1:
                        invert(t, p - 1)
                    if t.first == 0:
                        for m in MESSAGES[p]:
                            copy_h0(m)
                    if t.first >= 1 and p == 4:
                        log_pows(t.row - 1)
                        copy_hid(t.row - 1)
                        exp_pows(t.row - 1)
                    if n >= 2:
                        weigh(t, p - 2)
                    if n == 1:
                        std_rows()
                    elif n > 1:
                        invert(t, p - 1)

            nc.scalar.preload_act_table_set("natural_log_exp_and_others")
            act.wait_ge(small_mm, 1)
            nc.scalar.copy(w1t[:], acc_late[:, 0:D])
            nc.scalar.copy(b_all[:], acc_once[:, 0:D]).then_inc(small_copied, 1)
            turns(act, turn, PHASES)
            end = Turn(G, 0, G)
            log(end, -1)
            weigh(end, -2)
            invert(end, -1)
            weigh(end, -1)
            log_pows(G - 1)
            copy_hid(G - 1)
            exp_pows(G - 1)

        @block.vector
        def _(dve):
            def row_sum(t, p):
                n = t.first * G + p
                dve.wait_ge(raw_loaded[p % RAW], (n // RAW + 1) * 16 + t.w * (16 * G // RAW))
                if p == 0 and t.first >= 1:
                    dve.wait_ge(rows_summed, t.row)
                nc.vector.tensor_reduce(rowpart[:, :, p:p + 1], raw[:, p % RAW], AX_X, ALU.add).then_inc(summed, 1)
                if p == G - 1:
                    dve.wait_ge(summed, t.blocks(p + 1))
                    if t.first >= 1:
                        dve.wait_ge(pows_ln, t.row)
                    nc.vector.tensor_reduce(pows[:, 0, :], rowpart[:], AX_X, ALU.add).then_inc(rows_summed, 1)

            def cut(t, p):
                v = kept[:, p % KEPT]
                dve.wait_ge(copied, t.blocks(p + 1, 2))
                if t.first * G + p >= WTS:
                    dve.wait_ge(acc0_done, t.blocks(p - WTS + 1))
                nc.vector.scalar_tensor_tensor(out=wt[:, p % WTS], in0=v, scalar=CUTOFF, in1=v, op0=ALU.is_lt,
                                               op1=ALU.mult).then_inc(cut_done, 1)

            def quad(t, p):
                v = wt[:, p % WTS]
                dve.wait_ge(inv_done, t.blocks(p + 1))
                nc.vector.scalar_tensor_tensor(out=v, in0=v, scalar=-2.0, in1=v, op0=ALU.add,
                                               op1=ALU.mult).then_inc(quad_done, 1)

            def add_sum(t, i):
                _, r, bank = ADDS[t.known][i]
                if r == "once":
                    dve.wait_ge(once_done, t.tally(at_once, G) + 1)
                    acc, row = acc_once, t.row
                else:
                    nth = sum(a[1] != "once" for a in ADDS[t.known][:i])
                    j = [j for j, job in enumerate(LATE[t.known]) if job[4]][nth]
                    dve.wait_ge(late_done, t.tally(lambda k: per_step(LATE, k)) + LATE_SLOTS + j + 1)
                    acc, row = (acc_late, side)[bank], t.w * SHARE[t.known] + r
                dve.wait_ge(added, t.tally(lambda k: per_step(ADDS, k)) + i + 1)
                rows = mixed[:, bass.ds(row, 1), :] if not isinstance(row, int) else mixed[:, row:row + 1, :]
                nc.vector.tensor_tensor(rows, acc[:].rearrange("d (a i) -> d a i", a=1), rows,
                                        ALU.add).then_inc(added, 1)

            def copy_x1t(g):
                dve.wait_ge(acc0_done, (g + 1) * G)
                nc.vector.tensor_copy(x1t[:], acc0[:]).then_inc(x1t_copied, 1)

            def make_x1(g):
                dve.wait_ge(x1_turned, g + 1)
                dve.wait_ge(x1_kept, g + 1)
                rows = x1[:, bass.ds(g * T, T), :]
                nc.vector.tensor_tensor(x1_now[:], side[:].rearrange("p (a d) -> p a d", a=T), rows,
                                        ALU.add).then_inc(x1_done, 1)
                dve.wait_ge(x1_done, g + 1)
                for a in range(T):
                    last = nc.vector.bn_stats(bn[:, a, :], x1_now[:, a, :])
                last.then_inc(stats_done, 1)

            def make_hid(g):
                dve.wait_ge(rows_summed, g + 1)
                dve.wait_ge(stats_done, g + 1)
                nc.vector.tensor_scalar(pows[:, 0, :], pows[:, 0, :], 1.0, None, ALU.add)
                for a in range(T):
                    last = nc.vector.bn_aggr(mv[:, a, :], bn[:, a, :])
                last.then_inc(moments_done, 1)
                dve.wait_ge(moments_done, g + 1)
                for a in range(T):
                    last = nc.vector.tensor_scalar(hid[:, a, :], x1_now[:, a, :], mv[:, a, 0:1], 0.0,
                                                   ALU.subtract, ALU.max)
                last.then_inc(hid_done, 1)
                nc.vector.tensor_scalar(pows[:, 1, :], mv[:, 0:T, 1], EPS, None, ALU.add).then_inc(pows_done, 1)

            def newton_step(y, a, tmp, done, before):
                nc.vector.tensor_tensor(tmp, y, y, ALU.mult).then_inc(done, 1)
                dve.wait_ge(done, before + 1)
                nc.vector.scalar_tensor_tensor(out=tmp, in0=tmp, scalar=-0.5, in1=a, op0=ALU.mult,
                                               op1=ALU.mult).then_inc(done, 1)
                dve.wait_ge(done, before + 2)
                nc.vector.scalar_tensor_tensor(out=y, in0=tmp, scalar=1.5, in1=y, op0=ALU.add,
                                               op1=ALU.mult).then_inc(done, 1)
                dve.wait_ge(done, before + 3)

            def make_support(g):
                dve.wait_ge(pows_exp, g + 1)
                newton_step(inv[:], pows[:], tmp1[:], newton, g * 3)
                nc.vector.tensor_copy(dinv[:, bass.ds(g * T, T)], inv[:, 0, :]).then_inc(dinv_done, 1)
                nc.vector.tensor_tensor(scale[:], inv[:, 0, :], inv[:, 1, :], ALU.mult).then_inc(scale_done, 1)
                dve.wait_ge(scale_done, g + 1)
                dve.wait_ge(sup_multiplied, g + 1)
                for a in range(T):
                    last = nc.vector.tensor_scalar(support[:, bass.ds(g * T + a, 1), :], side[:, a * P:(a + 1) * P],
                                                   scale[:, a:a + 1], None, ALU.mult)
                last.then_inc(sup_done, 1)

            def take_moments(i):
                dve.wait_ge(x_loaded[i], 16)
                for a in range(i * NT // X_PARTS, (i + 1) * NT // X_PARTS):
                    last = nc.vector.bn_stats(bn[:, a, :], x1[:, a, :])
                if i < X_PARTS - 1:
                    return
                last.then_inc(bn_all, 1)
                dve.wait_ge(bn_all, 1)
                for a in range(NT):
                    last = nc.vector.bn_aggr(mv[:, a, :], bn[:, a, :])
                last.then_inc(mv_all, 1)
                dve.wait_ge(mv_all, 1)
                for a in range(ORDER[0] * T, ORDER[0] * T + T):
                    last = nc.vector.tensor_scalar(support[:, a, :], x1[:, a, :], mv[:, a, 0:1], 0.0,
                                                   ALU.subtract, ALU.max)
                last.then_inc(h0_done, 1)
                nc.vector.tensor_scalar(var0[:], mv[:, :, 1], EPS, None, ALU.add).then_inc(var_all, 1)

            def make_msg(p):
                dve.wait_ge(m_multiplied, p + 1)
                for a in range(T):
                    n = ORDER[p] * T + a
                    last = nc.vector.scalar_tensor_tensor(out=msg[:, n, :], in0=msg_banks[p % 2][:, a * P:(a + 1) * P],
                                                          scalar=rs0[:, n:n + 1], in1=b_all[:], op0=ALU.mult,
                                                          op1=ALU.add)
                last.then_inc(msg_done, 1)

            def turn(t):
                for p in range(G):
                    n = t.first * G + p
                    if n >= 2:
                        quad(t, p - 2)
                    for i, a in enumerate(ADDS[t.known]):
                        if a[0] == p:
                            add_sum(t, i)
                    row_sum(t, p)
                    if t.first >= 1 and p == 2:
                        copy_x1t(t.row - 1)
                    if n == 0:
                        take_moments(0)
                    if t.first >= 1 and p == 3:
                        make_x1(t.row - 1)
                    cut(t, p)
                    if t.first >= 1 and p == 3:
                        make_hid(t.row - 1)
                    if t.first >= 1 and p == 4:
                        make_support(t.row - 1)
                    if n == 0:
                        for i in range(1, X_PARTS):
                            take_moments(i)
                    if n == 1:
                        dve.wait_ge(exp_all, 1)
                        newton_step(rs0[:], var0[:], tmp0[:], newton_all, 0)
                        dve.wait_ge(small_copied, 1)
                    if t.first == 0:
                        for m in MESSAGES[p]:
                            make_msg(m)
                for i, a in enumerate(ADDS[t.known]):
                    if a[0] == G:
                        add_sum(t, i)

            turns(dve, turn, PHASES)

            end = Turn(G, 0, G)
            quad(end, -2)
            quad(end, -1)
            copy_x1t(G - 1)
            make_x1(G - 1)
            make_hid(G - 1)
            make_support(G - 1)

            def add_end(r):
                dve.wait_ge(late_done, NUM_LATE + LATE_SLOTS + 1 + END.index((r, G - 1)))
                dve.wait_ge(added, NUM_ADDS + 1)
                if r >= 2:
                    dve.wait_ge(mix_turned, r - 1)
                nc.vector.tensor_tensor(mix_end[:, r % 2, :], turned_ps[:, r % T, :], mixed[:, r, :],
                                        ALU.add).then_inc(end_added, 1)

            def finish(r):
                dve.wait_ge(mix_turned, r + 1)
                if r == 0:
                    dve.wait_ge(x1_kept, G + 1)
                    dve.wait_ge(sup_done, G)
                    dve.wait_ge(dinv_done, G)
                if r >= 2:
                    dve.wait_ge(out_written[r % 2], 16 * (r // 2))
                rows = slice(r * T, r * T + T)
                bank = (acc_once, acc_late)[r % 2]
                nc.vector.tensor_tensor(fin[:, r % 2], bank[:].rearrange("p (a d) -> p a d", a=T),
                                        support[:, rows, :], ALU.add).then_inc(out_summed, 1)
                dve.wait_ge(out_summed, r + 1)
                for a in range(T):
                    last = nc.vector.tensor_scalar(fin[:, r % 2, a, :], fin[:, r % 2, a, :],
                                                   dinv[:, r * T + a:r * T + a + 1], 0.0, ALU.mult, ALU.max)
                last.then_inc(out_relu, 1)
                dve.wait_ge(out_relu, r + 1)
                nc.vector.tensor_tensor(fin[:, r % 2], fin[:, r % 2], x1[:, rows, :], ALU.add).then_inc(out_done, 1)

            for r in range(G):
                add_end(r)
                if r >= 1:
                    finish(r - 1)
            finish(G - 1)


_INS = ["x", "adj", "L0_gnn_W", "L0_gnn_B", "L1_gnn_W"]


def kernel(**inputs):
    import numpy as _np
    import concourse.bacc as _bacc
    from concourse import mybir as _mybir
    from concourse.bass_utils import run_bass_kernel_spmd as _run

    nc = _bacc.Bacc("TRN2", target_bir_lowering=False, num_devices=1)
    arrays, args = {}, []
    for name in _INS:
        a = _np.ascontiguousarray(inputs[name])
        arrays[f"in_{name}_dram"] = a
        args.append(nc.dram_tensor(f"in_{name}_dram", a.shape, _mybir.dt.from_np(a.dtype), kind="ExternalInput").ap())
    shape = inputs["x"].shape
    args.append(nc.dram_tensor("out_0_dram", shape, _mybir.dt.float32, kind="ExternalOutput").ap())
    build(nc, *args)
    r = _run(nc, [arrays], core_ids=[0])
    return r.results[0]["out_0_dram"]
```
